# Optimizing a Trainium2 kernel written in Bass

```python
import numpy as np
import jax
import jax.numpy as jnp

def _softmax(x, axis=-1):
    return jax.nn.softmax(x, axis=axis)

def _gelu(x):
    return jax.nn.gelu(x, approximate=True)

def _silu(x):
    return jax.nn.silu(x)

def _sigmoid(x):
    return jax.nn.sigmoid(x)

def _layernorm(x, axis=-1, eps=1e-05):
    m = jnp.mean(x, axis=axis, keepdims=True)
    v = jnp.var(x, axis=axis, keepdims=True)
    return (x - m) / jnp.sqrt(v + eps)

def _scatter_add(tgt, idx, src, axis=0):
    return tgt.at[idx].add(src)

def _segment_sum(src, seg, n):
    return jax.ops.segment_sum(src, seg, n)
kernel_name = 'mk_metaformer_d2_conv_nchw256_r4_e4d76e'

def setup_inputs(seed: int=0):
    np.random.seed(seed)
    _w = jnp.asarray

    def _rec_inputs():
        import jax
        import jax.numpy as jnp
        _gk = jax.random.key(seed)
        x = -0.0003482 + 1 * jax.random.normal(jax.random.fold_in(_gk, 1), (8, 64, 24, 24), jnp.float32)
        return x
    x = _rec_inputs()

    def _L0_conv_setup():
        import jax, jax.numpy as jnp
        import numpy as np
        BN_EPS = 1e-05
        L1_EPS = 1e-12

        def _bn(x, gamma, beta, mean, var):
            inv = gamma / jnp.sqrt(var + BN_EPS)
            return x * inv[None, :, None, None] + (beta - mean * inv)[None, :, None, None]
        key = jax.random.key(seed)
        ks = jax.random.split(key, 12)
        B, Cin, H, W = (8, 64, 24, 24)
        mid = 32
        P = mid * (mid - 1) // 2
        out = Cin
        x0 = jax.random.normal(ks[0], (B, Cin, H, W), dtype=jnp.float32)
        w11 = jax.random.normal(ks[1], (mid, Cin), dtype=jnp.float32) * 0.05
        g1 = 1.0 + 0.1 * jax.random.normal(ks[2], (mid,), dtype=jnp.float32)
        b1 = 0.1 * jax.random.normal(ks[3], (mid,), dtype=jnp.float32)
        m1 = 0.1 * jax.random.normal(ks[4], (mid,), dtype=jnp.float32)
        v1 = jax.random.uniform(ks[5], (mid,), dtype=jnp.float32, minval=0.5, maxval=1.5)
        w12 = jax.random.normal(ks[6], (out, P), dtype=jnp.float32) * 0.05
        g2 = 1.0 + 0.1 * jax.random.normal(ks[7], (out,), dtype=jnp.float32)
        b2 = 0.1 * jax.random.normal(ks[8], (out,), dtype=jnp.float32)
        m2 = 0.1 * jax.random.normal(ks[9], (out,), dtype=jnp.float32)
        v2 = jax.random.uniform(ks[10], (out,), dtype=jnp.float32, minval=0.5, maxval=1.5)
        kf = jax.random.split(ks[11], 2)
        wfc = jax.random.normal(kf[0], (out, 2 * out), dtype=jnp.float32) * 0.05
        bfc = 0.02 * jax.random.normal(kf[1], (out,), dtype=jnp.float32)
        return {'x0': x0, 'w11': w11, 'g1': g1, 'b1': b1, 'm1': m1, 'v1': v1, 'w12': w12, 'g2': g2, 'b2': b2, 'm2': m2, 'v2': v2, 'wfc': wfc, 'bfc': bfc}
    _L0_conv_all = _L0_conv_setup()
    _L0_conv_in = {k: v for k, v in _L0_conv_all.items() if k in ('w11', 'g1', 'b1', 'm1', 'v1', 'w12', 'g2', 'b2', 'm2', 'v2', 'wfc', 'bfc')}
    del _L0_conv_all

    def _L0_ffn_setup():
        import math
        import jax, jax.numpy as jnp
        import numpy as np
        CAPACITY_FACTOR = 1.25
        TOP_K = 2
        LN_EPS = 1e-05

        def _layer_norm(x, gamma, beta):
            mu = jnp.mean(x, axis=-1, keepdims=True)
            var = jnp.var(x, axis=-1, keepdims=True)
            return (x - mu) * jax.lax.rsqrt(var + LN_EPS) * gamma + beta
        key = jax.random.key(seed)
        ks = jax.random.split(key, 4)
        B, S, D, F, E = (8, 1024, 64, 128, 8)
        x = jax.random.normal(ks[0], (B, S, D), dtype=jnp.float32)
        Wr = jax.random.normal(ks[1], (D, E), dtype=jnp.float32) / np.sqrt(D)
        br = jnp.zeros((E,), jnp.float32)
        W1 = jax.random.normal(ks[2], (E, D, F), dtype=jnp.float32) / np.sqrt(D)
        b1 = jnp.zeros((E, F), jnp.float32)
        W2 = jax.random.normal(ks[3], (E, F, D), dtype=jnp.float32) / np.sqrt(F)
        b2 = jnp.zeros((E, D), jnp.float32)
        gamma = jnp.ones((D,), jnp.float32)
        beta = jnp.zeros((D,), jnp.float32)
        return {'x': x, 'Wr': Wr, 'br': br, 'W1': W1, 'b1': b1, 'W2': W2, 'b2': b2, 'gamma': gamma, 'beta': beta}
    _L0_ffn_all = _L0_ffn_setup()
    _L0_ffn_in = {k: v for k, v in _L0_ffn_all.items() if k in ('Wr', 'br', 'W1', 'b1', 'W2', 'b2', 'gamma', 'beta')}
    del _L0_ffn_all

    def _L1_conv_setup():
        import jax, jax.numpy as jnp
        import numpy as np
        IC, OC, K = (64, 64, 3)
        key = jax.random.key(seed)
        kx, kw = jax.random.split(key)
        x = jax.random.normal(kx, (32, IC, 56, 56), dtype=jnp.float32)
        w = jnp.clip(jax.random.normal(kw, (OC, IC, K, K), dtype=jnp.float32), -2.0, 2.0) * 0.1
        return {'x': x, 'w': w}
    _L1_conv_all = _L1_conv_setup()
    _L1_conv_in = {k: v for k, v in _L1_conv_all.items() if k in ('w',)}
    del _L1_conv_all

    def _L1_ffn_setup():
        import jax, jax.numpy as jnp
        import numpy as np
        TOP_K = 2
        key = jax.random.key(seed)
        ks = jax.random.split(key, 4)
        B, L, D, H, E = (8, 1024, 64, 256, 8)
        s = 0.02
        return {'x': jax.random.normal(ks[0], (B, L, D), jnp.float32), 'Wg': jax.random.normal(ks[1], (D, E), jnp.float32) * s, 'bg': jnp.zeros((E,), jnp.float32), 'W1': jax.random.normal(ks[2], (E, D, H), jnp.float32) * s, 'b1': jnp.zeros((E, H), jnp.float32), 'W2': jax.random.normal(ks[3], (E, H, D), jnp.float32) * s, 'b2': jnp.zeros((E, D), jnp.float32)}
    _L1_ffn_all = _L1_ffn_setup()
    _L1_ffn_in = {k: v for k, v in _L1_ffn_all.items() if k in ('Wg', 'bg', 'W1', 'b1', 'W2', 'b2')}
    del _L1_ffn_all
    return {'x': x, 'L0_conv_w11': _L0_conv_in['w11'], 'L0_conv_g1': _L0_conv_in['g1'], 'L0_conv_b1': _L0_conv_in['b1'], 'L0_conv_m1': _L0_conv_in['m1'], 'L0_conv_v1': _L0_conv_in['v1'], 'L0_conv_w12': _L0_conv_in['w12'], 'L0_conv_g2': _L0_conv_in['g2'], 'L0_conv_b2': _L0_conv_in['b2'], 'L0_conv_m2': _L0_conv_in['m2'], 'L0_conv_v2': _L0_conv_in['v2'], 'L0_conv_wfc': _L0_conv_in['wfc'], 'L0_conv_bfc': _L0_conv_in['bfc'], 'L0_ffn_Wr': _L0_ffn_in['Wr'], 'L0_ffn_br': _L0_ffn_in['br'], 'L0_ffn_W1': _L0_ffn_in['W1'], 'L0_ffn_b1': _L0_ffn_in['b1'], 'L0_ffn_W2': _L0_ffn_in['W2'], 'L0_ffn_b2': _L0_ffn_in['b2'], 'L0_ffn_gamma': _L0_ffn_in['gamma'], 'L0_ffn_beta': _L0_ffn_in['beta'], 'L1_conv_w': _L1_conv_in['w'], 'L1_ffn_Wg': _L1_ffn_in['Wg'], 'L1_ffn_bg': _L1_ffn_in['bg'], 'L1_ffn_W1': _L1_ffn_in['W1'], 'L1_ffn_b1': _L1_ffn_in['b1'], 'L1_ffn_W2': _L1_ffn_in['W2'], 'L1_ffn_b2': _L1_ffn_in['b2']}

def reference(x, L0_conv_w11, L0_conv_g1, L0_conv_b1, L0_conv_m1, L0_conv_v1, L0_conv_w12, L0_conv_g2, L0_conv_b2, L0_conv_m2, L0_conv_v2, L0_conv_wfc, L0_conv_bfc, L0_ffn_Wr, L0_ffn_br, L0_ffn_W1, L0_ffn_b1, L0_ffn_W2, L0_ffn_b2, L0_ffn_gamma, L0_ffn_beta, L1_conv_w, L1_ffn_Wg, L1_ffn_bg, L1_ffn_W1, L1_ffn_b1, L1_ffn_W2, L1_ffn_b2):
    import jax
    import jax.numpy as jnp

    def _L0_conv_ref(x0, w11, g1, b1, m1, v1, w12, g2, b2, m2, v2, wfc, bfc):
        import jax, jax.numpy as jnp
        import numpy as np
        BN_EPS = 1e-05
        L1_EPS = 1e-12

        def _bn(x, gamma, beta, mean, var):
            inv = gamma / jnp.sqrt(var + BN_EPS)
            return x * inv[None, :, None, None] + (beta - mean * inv)[None, :, None, None]
        x = jnp.einsum('bchw,oc->bohw', x0, w11)
        x = jax.nn.relu(_bn(x, g1, b1, m1, v1))
        l1 = jnp.sum(jnp.abs(x), axis=1, keepdims=True)
        x = x / jnp.maximum(l1, L1_EPS)
        C = x.shape[1]
        iu0, iu1 = np.triu_indices(C, k=1)
        gram = x[:, iu0] * x[:, iu1]
        y = jnp.einsum('bphw,op->bohw', gram, w12)
        y = jax.nn.relu(_bn(y, g2, b2, m2, v2))
        cat = jnp.concatenate((y, x0), axis=1)
        return jnp.einsum('bchw,oc->bohw', cat, wfc) + bfc[None, :, None, None]

    def _L0_ffn_ref(x, Wr, br, W1, b1, W2, b2, gamma, beta):
        import math
        import jax, jax.numpy as jnp
        import numpy as np
        CAPACITY_FACTOR = 1.25
        TOP_K = 2
        LN_EPS = 1e-05

        def _layer_norm(x, gamma, beta):
            mu = jnp.mean(x, axis=-1, keepdims=True)
            var = jnp.var(x, axis=-1, keepdims=True)
            return (x - mu) * jax.lax.rsqrt(var + LN_EPS) * gamma + beta
        B, S, D = x.shape
        E = Wr.shape[1]
        N = B * S
        K = TOP_K
        logits = jnp.mean(x, axis=1) @ Wr + br
        routing_weights = jax.nn.softmax(logits, axis=-1)
        capacity = float(math.ceil(N * CAPACITY_FACTOR / E))
        expected_loads = routing_weights.sum(axis=0) * (N / B)
        scale = jnp.where(expected_loads > capacity, capacity / expected_loads, 1.0)
        routing_weights = jax.nn.softmax(routing_weights * scale, axis=-1)
        rw_tok = jnp.broadcast_to(routing_weights[:, None, :], (B, S, E)).reshape(N, E)
        top_w, top_i = jax.lax.top_k(rw_tok, K)
        top_w = jax.nn.softmax(top_w, axis=-1)
        xf = x.reshape(N, D)
        h = jax.nn.gelu(jnp.einsum('nd,edf->enf', xf, W1) + b1[:, None, :], approximate=False)
        y = jnp.einsum('enf,efd->end', h, W2) + b2[:, None, :]
        w_dense = jnp.zeros((N, E), x.dtype).at[jnp.arange(N)[:, None], top_i].add(top_w)
        out = jnp.einsum('ne,end->nd', w_dense, y).reshape(B, S, D)
        out = _layer_norm(out + x, gamma, beta)
        return out

    def _L1_conv_ref(x, w):
        import jax, jax.numpy as jnp
        import numpy as np
        IC, OC, K = (64, 64, 3)
        k = w.shape[-1]
        pad = (k - 1) // 2
        out = jax.lax.conv_general_dilated(x, w, window_strides=(1, 1), padding=((pad, pad), (pad, pad)), dimension_numbers=('NCHW', 'OIHW', 'NCHW'))
        return out / (k * k)

    def _L1_ffn_ref(x, Wg, bg, W1, b1, W2, b2):
        import jax, jax.numpy as jnp
        import numpy as np
        TOP_K = 2
        B, L, D = x.shape
        E = W1.shape[0]
        xf = x.reshape(-1, D)
        gate_logits = xf @ Wg + bg
        top_w, top_i = jax.lax.top_k(gate_logits, TOP_K)
        top_w = jax.nn.softmax(top_w, axis=-1)
        w_dense = jnp.sum(jax.nn.one_hot(top_i, E, dtype=xf.dtype) * top_w[..., None], axis=1)
        out = jnp.zeros_like(xf)
        for e in range(E):
            h = jax.nn.gelu(xf @ W1[e] + b1[e], approximate=False)
            out = out + w_dense[:, e:e + 1] * (h @ W2[e] + b2[e])
        return out.reshape(B, L, D)

    def _gn(v, G=32, eps=1e-05):
        B_, C_, H_, W_ = v.shape
        g = v.reshape(B_, G, C_ // G, H_, W_)
        m = jnp.mean(g, axis=(2, 3, 4), keepdims=True)
        s = jnp.var(g, axis=(2, 3, 4), keepdims=True)
        return ((g - m) / jnp.sqrt(s + eps)).reshape(v.shape)

    def _ln_c(v, eps=1e-06):
        m = jnp.mean(v, axis=1, keepdims=True)
        s = jnp.var(v, axis=1, keepdims=True)
        return (v - m) / jnp.sqrt(s + eps)

    def _ln_t(v, eps=1e-05):
        m = jnp.mean(v, axis=-1, keepdims=True)
        s = jnp.var(v, axis=-1, keepdims=True)
        return (v - m) / jnp.sqrt(s + eps)

    def _to_tokens(v):
        B_, C_, H_, W_ = v.shape
        return v.reshape(B_, C_, H_ * W_).transpose(0, 2, 1)

    def _from_tokens(t, like):
        B_, C_, H_, W_ = like.shape
        return t.transpose(0, 2, 1).reshape(B_, C_, H_, W_)
    x = x + _L0_conv_ref(_ln_c(x), L0_conv_w11, L0_conv_g1, L0_conv_b1, L0_conv_m1, L0_conv_v1, L0_conv_w12, L0_conv_g2, L0_conv_b2, L0_conv_m2, L0_conv_v2, L0_conv_wfc, L0_conv_bfc)
    t = _to_tokens(x)
    t = t + _L0_ffn_ref(_ln_t(t), L0_ffn_Wr, L0_ffn_br, L0_ffn_W1, L0_ffn_b1, L0_ffn_W2, L0_ffn_b2, L0_ffn_gamma, L0_ffn_beta)
    x = _from_tokens(t, x)
    x = x + _L1_conv_ref(_ln_c(x), L1_conv_w)
    t = _to_tokens(x)
    t = t + _L1_ffn_ref(_ln_t(t), L1_ffn_Wg, L1_ffn_bg, L1_ffn_W1, L1_ffn_b1, L1_ffn_W2, L1_ffn_b2)
    x = _from_tokens(t, x)
    return x

_drawn_inputs = setup_inputs


def setup_inputs(seed=0):
    import zlib

    import numpy as np

    out = dict(_drawn_inputs(seed))
    spreads = {'L0_ffn_br': (0.0, 0.1),
     'L0_ffn_b1': (0.0, 0.385),
     'L0_ffn_b2': (0.0, 0.1),
     'L0_ffn_gamma': (1.0, 0.2),
     'L0_ffn_beta': (0.0, 0.1),
     'L1_ffn_bg': (0.0, 0.276),
     'L1_ffn_b1': (0.0, 0.8),
     'L1_ffn_b2': (0.0, 0.1)}
    factors = {'L0_conv_w11': 8.0,
     'L0_conv_g1': 8.0,
     'L0_conv_b1': 8.0,
     'L0_conv_m1': 8.0,
     'L0_conv_v1': 8.0,
     'L0_conv_w12': 8.0,
     'L0_conv_g2': 8.0,
     'L0_conv_v2': 8.0,
     'L0_conv_bfc': 2.675,
     'L0_ffn_Wr': 8.0,
     'L1_ffn_W1': 6.38,
     'L1_ffn_W2': 5.36}
    for name, (base, spread) in spreads.items():
        noise = np.random.default_rng([zlib.crc32(name.encode()), seed]).standard_normal(out[name].shape)
        drawn = base * np.exp(spread * noise) if base else spread * noise
        out[name] = jnp.asarray(drawn.astype(out[name].dtype))
    for name, factor in factors.items():
        out[name] = (out[name] * factor).astype(out[name].dtype)
    return out
```

```python
from contextlib import ExitStack

import numpy as np

import concourse.bass as bass
from concourse import mybir

BATCH, CH, HT, WD = 8, 64, 24, 24
PIX = HT * WD
MID = 32
EXP = 8
F0 = 128
F1 = 256
HID = F1 // 128
PAIRS = BATCH // 2
COLS = PAIRS * PIX
CHUNK = 768
NCH = COLS // CHUNK
BANK = CHUNK // 2
TILE = 128
TPC = CHUNK // TILE
NT = COLS // TILE
HALFPIX = PIX // 2
ROWS = HT // 2
GT = 4
TAPS = 9
PADW = WD + 2
PADN = (HT + 2) * PADW
CAPACITY = -(-BATCH * PIX * 5 // (4 * EXP))
UNITS = EXP * HID

F32 = mybir.dt.float32
F32R = mybir.dt.float32r
I32 = mybir.dt.int32
ALU = mybir.AluOpType
ACT = mybir.ActivationFunctionType
AX = mybir.AxisListType.X

EARLY = {
    "center": 128, "blockmean": 2, "ident": 128, "w11": 128, "bn1": 4, "bn2": 4, "bfc": 1,
    "l1sum": 2, "perm": GT * 128, "w12": GT * CH, "wfcy": 128, "wfcx": 128,
}
MIX0 = {
    "wr": EXP, "br": EXP, "below": EXP * EXP, "above": EXP * EXP, "iota": EXP, "eye8": 8, "diag": 16,
    "ones8": 128, "b2": CH, "gamma": 1, "beta": 1, "w1": EXP * F0, "w2b1": EXP * (CH + 1),
}
LATE = {
    "conv": TAPS * CH, "wg": EXP, "bg": EXP, "spread": EXP * 128, "b1": UNITS, "b2": EXP,
    "w1": EXP * F1, "w2": UNITS * CH,
}


def places(table):
    out, at = {}, 0
    for name, n in table.items():
        out[name] = (at, at + n)
        at += n
    return out, at


RT_L1, RT_SOFT1, RT_L2, RT_DIFF, RT_PICKED, RT_IDX, RT_WDT, RT_B2 = 5, 7, 11, 30, 37, 39, 40, 41
GT_EXP, GT_DONE = 3, 37


def pieces(c):
    out, a = [], c * CHUNK
    while a < (c + 1) * CHUNK:
        p, y0 = a // PIX, a % PIX // WD
        ny = min(HT - y0, ((c + 1) * CHUNK - a) // WD)
        out.append((a - c * CHUNK, p, y0, ny))
        a += ny * WD
    return out


def build(nc, x, early_in, mix0_in, late_in, out):
    at_e, n_e = places(EARLY)
    at_m, n_m = places(MIX0)
    at_l, n_l = places(LATE)
    ctx = ExitStack()
    with ctx:
        def sb(name, shape, dt=F32):
            return ctx.enter_context(nc.sbuf_tensor(name, shape, dt))

        def sem(name):
            return ctx.enter_context(nc.semaphore(name))

        early = sb("early", [128, n_e])
        mix0 = sb("mix0", [128, n_m])
        late = sb("late", [128, n_l])

        def E(name, rows=128):
            return early[0:rows, at_e[name][0]:at_e[name][1]]

        def M(name, rows=128):
            return mix0[0:rows, at_m[name][0]:at_m[name][1]]

        def L(name, rows=128):
            return late[0:rows, at_l[name][0]:at_l[name][1]]

        w11_hl = sb("w11_hl", [128, 2, 128], F32R)
        perm_r = sb("perm_r", [128, GT, 128], F32R)
        l1sum_r = sb("l1sum_r", [128, 2], F32R)
        w1m_hl = sb("w1m_hl", [128, EXP, 2, F0], F32R)
        conv_hl = sb("conv_hl", [128, TAPS, 2, CH], F32R)
        wg_hl = sb("wg_hl", [128, 2, EXP], F32R)
        spread_r = sb("spread_r", [48, EXP, 128], F32R)
        w1_h = sb("w1_h", [128, EXP * F1], F32R)
        w1_l = sb("w1_l", [128, EXP * F1], F32R)

        X = sb("X", [128, COLS])
        D = sb("D", [128, COLS])
        Q = sb("Q", [128, COLS])
        N = sb("N", [128, COLS])
        XS = sb("XS", [128, 2, COLS], F32R)
        dev = sb("dev", [128, NT * 2])
        rdev = sb("rdev", [128, NT * 2])
        eps = sb("eps", [128, 2])
        bnw = sb("bnw", [128, 8])
        amp = sb("amp", [128, 2, COLS])
        amp_s = sb("amp_s", [128, 2, COLS], F32R)
        rl1 = sb("rl1", [128, NT * 2])
        rl1sq = sb("rl1sq", [128, NT * 2])
        gram = sb("gram", [128, 4, CHUNK])
        w1sel = amp_s[:, :, :].rearrange("p a n -> p (a n)")[:, 0:BATCH * 4 * F0].rearrange(
            "p (b k q f) -> p b k q f", b=BATCH, k=2, q=2)
        h0 = amp[:, 0, :].rearrange("p (s n) -> p s n", s=4)
        gB = amp[:, 0, 0:2 * CHUNK].rearrange("p (s n) -> p s n", s=2)
        tmp = amp[:, 0, 2 * CHUNK:3 * CHUNK]
        clow = amp[:, 1, :]
        h1 = gram
        yraw = sb("yraw", [128, COLS])
        imsum = sb("imsum", [128, PAIRS])
        msum = sb("msum", [128, BATCH])
        r8 = sb("r8", [8, 16, 8])
        r88 = sb("r88", [8, 4, 64])
        pick = sb("pick", [8, 2, 8])
        pickv = sb("pickv", [8, 4])
        pickd = sb("pickd", [8, 2, BATCH, 2])
        pickb = sb("pickb", [128, 2 * BATCH * 2])
        picki = sb("picki", [1, BATCH * 2], I32)
        wdT = sb("wdT", [8, 8])
        b2sel = sb("b2sel", [128, PAIRS])
        w2sel = sb("w2sel", [128, BATCH, 2, CH])
        b1sel = sb("b1sel", [128, BATCH, 2])
        img = sb("img", [128, BATCH, PADN], F32R)
        lg, rank, gcmp, gw = (yraw[:, q * NT * 2 * EXP:(q + 1) * NT * 2 * EXP].rearrange("p (n e) -> p n e", e=EXP)
                              for q in range(4))
        gmx = sb("gmx", [128, 3, NT * 2])
        gT = img[:, :, :].rearrange("p b n -> p (b n)")[0:48, 0:COLS]

        PS = ctx.enter_context(nc.psum_tensor("PS", [128, 8, 512], F32))

        def pair(k, n=BANK, lo=0, hi=128):
            return PS[lo:hi, 2 * k:2 * k + 2, 0:n]

        def cols(t, c, lo=0, hi=128):
            return t[lo:hi, c * CHUNK:(c + 1) * CHUNK].rearrange("p (j n) -> p j n", j=2)

        def icols(t, p, lo=0, hi=128):
            return t[lo:hi, p * PIX:(p + 1) * PIX].rearrange("p (j n) -> p j n", j=2)

        x_in = [sem(f"x_in{i}") for i in range(PAIRS)]
        early_ld, mix0_ld, late_ld = sem("early_ld"), sem("mix0_ld"), sem("late_ld")
        prep_r = sem("prep_r")
        prep_w11 = sem("prep_w11")
        bn_a, bn_b = sem("bn_a"), sem("bn_b")
        fold = sem("fold")
        epsset = sem("epsset")
        LN = [{k: sem(f"ln{i}_{k}") for k in
               ("centered", "squared", "copied", "summed", "rooted", "inverted", "spread", "normed", "high", "low")}
              for i in range(5)]
        amp_mm, amp_done = sem("amp_mm"), sem("amp_done")
        amp_hi, amp_lo = sem("amp_hi"), sem("amp_lo")
        l1_mm, l1_max, l1_inv, l1_sq, l1_bc = sem("l1_mm"), sem("l1_max"), sem("l1_inv"), sem("l1_sq"), sem("l1_bc")
        shift_mm, gram_done, y_mm, y_copied = sem("shift_mm"), sem("gram_done"), sem("y_mm"), sem("y_copied")
        y_scaled, y_act, fc_mm, x1_done = sem("y_scaled"), sem("y_act"), sem("fc_mm"), sem("x1_done")
        m0_hi, m0_lo = sem("m0_hi"), sem("m0_lo")
        rt, rt_pe, rt_act = sem("rt"), sem("rt_pe"), sem("rt_act")
        msum0 = sem("msum0")
        sel_w1, sel_w2, sel_b1 = sem("sel_w1"), sem("sel_w2"), sem("sel_b1")
        f0_mm, f0_act, f0_out, f0_res = sem("f0_mm"), sem("f0_act"), sem("f0_out"), sem("f0_res")
        xbeta, x2_done = sem("xbeta"), sem("x2_done")
        img0 = sem("img0")
        conv_w = sem("conv_w")
        conv_mm, conv_low, conv_a, x3_done = sem("conv_mm"), sem("conv_low"), sem("conv_a"), sem("x3_done")
        wg_s, w1_hs, w1_ls, spread_s = sem("wg_s"), sem("w1_hs"), sem("w1_ls"), sem("spread_s")
        lg_mm, gt, gt_act = sem("lg_mm"), sem("gt"), sem("gt_act")
        gT0, gT_mm, gT_hi, gT_lo = sem("gT0"), sem("gT_mm"), sem("gT_hi"), sem("gT_lo")
        f1_mm, f1_act, g_mm, g_act = sem("f1_mm"), sem("f1_act"), sem("g_mm"), sem("g_act")
        f1_out, o_mul, o_add = sem("f1_out"), sem("o_mul"), sem("o_add")
        stored = sem("stored")

        def chunks_for(p):
            return -(-(p + 1) * PIX // CHUNK)

        def images_for(c):
            return -(-(c + 1) * CHUNK // PIX)

        CEN, BC, SUM = [0, 1, 0], [2, 1, 0], [6, 7, 6]

        block = ctx.enter_context(nc.Block())

        @block.sync
        def _(sp):
            xv = x.rearrange("(h p) c y z -> p h c (y z)", h=2)
            ov = out.rearrange("(h p) c y z -> h c p (y z)", h=2)
            sp.dma_start(early[:, :], early_in).then_inc(early_ld, 16)
            for p in range(PAIRS):
                for half in range(2):
                    sp.dma_start(X[64 * half:64 * half + 64, p * PIX:(p + 1) * PIX], xv[p, half]).then_inc(x_in[p], 16)
            sp.dma_start(mix0[:, :], mix0_in).then_inc(mix0_ld, 16)
            sp.dma_start(late[:, :], late_in).then_inc(late_ld, 16)
            for p in range(PAIRS):
                sp.wait_ge(o_add, EXP * chunks_for(p))
                for half in range(2):
                    sp.dma_start(ov[half][:, p], X[64 * half:64 * half + 64, p * PIX:(p + 1) * PIX]).then_inc(stored, 16)
            sp.wait_ge(stored, 16 * 2 * PAIRS)

        @block.tensor
        def _(pe):
            def layer_norm(i, x_ready, first_free, second_free, third_free, sum_free):
                s = LN[i]

                def center(c):
                    x_ready(c)
                    if c == 0:
                        first_free()
                    if c == 1:
                        second_free()
                    if c == 2:
                        pe.wait_ge(s["squared"], 1)
                        pe.wait_ge(s["copied"], 1)
                    for j in range(2):
                        mm = pe.matmul(PS[:, 2 * CEN[c] + j, 0:BANK], E("center"),
                                       X[:, c * CHUNK + j * BANK:c * CHUNK + (j + 1) * BANK], start=True, stop=True)
                    mm.then_inc(s["centered"], 1)

                def sums(c):
                    pe.wait_ge(s["squared"], c + 1)
                    if c == 0:
                        sum_free()
                    if c == 2:
                        pe.wait_ge(s["rooted"], 1)
                    for t in range(TPC * c, TPC * c + TPC):
                        mm = pe.matmul(PS[:, SUM[c], 2 * t:2 * t + 2], Q[:, t * TILE:(t + 1) * TILE], E("blockmean"),
                                       start=True, stop=True)
                    mm.then_inc(s["summed"], 1)

                def spread(c):
                    pe.wait_ge(s["inverted"], c + 1)
                    if c == 0:
                        third_free()
                    else:
                        pe.wait_ge(s["squared"], c + 1)
                        pe.wait_ge(s["copied"], c + 1)
                    for k in range(TPC):
                        t = TPC * c + k
                        for half in range(2):
                            n = 2 * t + half
                            mm = pe.matmul(PS[64 * half:64 * half + 64, 2 * BC[c] + k // 3, (k % 3) * TILE:(k % 3 + 1) * TILE],
                                           rdev[:, n:n + 1].to_broadcast([128, CH]), E("ident"), start=True, stop=True,
                                           skip_group_check=True)
                    mm.then_inc(s["spread"], 1)

                center(0)
                center(1)
                sums(0)
                center(2)
                spread(0)
                sums(1)
                spread(1)
                sums(2)
                spread(2)

            def nothing():
                pass

            pe.wait_ge(early_ld, 16)

            def x_loaded(c):
                for p in range(images_for(c)):
                    pe.wait_ge(x_in[p], 32)

            layer_norm(0, x_loaded, nothing, nothing, nothing, nothing)

            pe.wait_ge(prep_w11, 2)
            for c in range(NCH):
                for half in range(2):
                    n = 2 * c + half
                    pe.wait_ge(LN[0]["high"], c + 1)
                    pe.wait_ge(LN[0]["low"], c + 1)
                    if n < 2:
                        pe.wait_ge(LN[0]["normed"], 3)
                    else:
                        pe.wait_ge(amp_done, n - 1)
                    for j in range(2):
                        a = c * CHUNK + j * BANK
                        for part in range(2):
                            mm = pe.matmul(PS[:, 2 * (n % 2) + j, 0:BANK], w11_hl[:, part, :], XS[:, half, a:a + BANK],
                                           start=part == 0, stop=part == 1)
                    mm.then_inc(amp_mm, 1)

            pe.wait_ge(prep_r, 2)
            pe.wait_ge(LN[0]["rooted"], 3)
            for c in range(NCH):
                pe.wait_ge(amp_lo, 2 * c + 2)
                pe.wait_ge(amp_hi, 2 * c + 2)
                if c == 2:
                    pe.wait_ge(l1_max, 1)
                for t in range(TPC * c, TPC * c + TPC):
                    for half in range(2):
                        mm = pe.matmul(PS[:, SUM[c], 4 * t + 2 * half:4 * t + 2 * half + 2],
                                       amp_s[:, half, t * TILE:(t + 1) * TILE], l1sum_r[:, :], start=True, stop=True)
                mm.then_inc(l1_mm, 1)

            def shifted(n):
                c, t, half = n // 8, n // 2 % 4, n % 2
                if n < 2:
                    pe.wait_ge(amp_done, 2 * NCH)
                else:
                    pe.wait_ge(gram_done, n - 1)
                for j in range(2):
                    a = c * CHUNK + j * BANK
                    mm = pe.matmul(PS[:, 2 * (n % 2) + j, 0:BANK], perm_r[:, t, :], amp_s[:, half, a:a + BANK],
                                   start=True, stop=True)
                mm.then_inc(shift_mm, 1)

            def products(c, t):
                pe.wait_ge(gram_done, 8 * c + 2 * t + 2)
                if t == 0:
                    if c == 0:
                        pe.wait_ge(LN[0]["normed"], 1)
                    else:
                        pe.wait_ge(y_copied, c)
                for j in range(2):
                    for half in range(2):
                        mm = pe.matmul(PS[64 * half:64 * half + 64, 4 + j, 0:BANK], E("w12").rearrange("p (t o) -> p t o", t=GT)[:, t],
                                       gram[:, 2 * (t % 2) + half, j * BANK:(j + 1) * BANK], start=t == 0, stop=t == GT - 1,
                                       skip_group_check=True)
                mm.then_inc(y_mm, 1)

            def spread_l1(c):
                pe.wait_ge(l1_sq, c + 1)
                pe.wait_ge(l1_max, NCH)
                if c > 0:
                    pe.wait_ge(y_scaled, c)
                for k in range(TPC):
                    t = TPC * c + k
                    for half in range(2):
                        n = 2 * t + half
                        mm = pe.matmul(PS[64 * half:64 * half + 64, 6 + k // 3, (k % 3) * TILE:(k % 3 + 1) * TILE],
                                       rl1sq[:, n:n + 1].to_broadcast([128, CH]), E("ident"), start=True, stop=True,
                                       skip_group_check=True)
                mm.then_inc(l1_bc, 1)

            total = 8 * NCH
            shifted(0)
            shifted(1)
            for c in range(NCH):
                for t in range(GT):
                    n = 8 * c + 2 * t
                    for k in (n + 2, n + 3):
                        if k < total:
                            shifted(k)
                    products(c, t)
                spread_l1(c)

            for c in range(NCH):
                pe.wait_ge(y_act, c + 1)
                if c == 0:
                    pe.wait_ge(gram_done, total)
                if c == 2:
                    pe.wait_ge(x1_done, 1)
                for j in range(2):
                    a = c * CHUNK + j * BANK
                    o = PS[:, 2 * (c % 2) + j, 0:BANK]
                    pe.matmul(o, E("wfcy"), yraw[:, a:a + BANK], start=True, stop=False)
                    mm = pe.matmul(o, E("wfcx"), N[:, a:a + BANK], start=False, stop=True)
                mm.then_inc(fc_mm, 1)

            layer_norm(1, lambda c: pe.wait_ge(x1_done, c + 1), lambda: pe.wait_ge(x1_done, 3), nothing,
                       lambda: pe.wait_ge(y_copied, NCH), lambda: pe.wait_ge(y_scaled, NCH))

            pe.wait_ge(mix0_ld, 16)
            pe.wait_ge(rt, 3)
            pe.wait_ge(LN[1]["rooted"], 3)
            pe.matmul(PS[0:8, 6, 0:8], msum[:, :], M("wr"), start=True, stop=True).then_inc(rt_pe, 1)
            pe.wait_ge(rt, RT_SOFT1)
            pe.matmul(PS[0:8, 6, 8:16], M("ones8", 8)[:, 0:8], r8[:, 4, :], start=True, stop=True).then_inc(rt_pe, 1)
            pe.wait_ge(rt, RT_PICKED)
            pe.matmul(PS[:, 6, 16:48], M("ones8", 8), pickd[:, :, :, :].rearrange("p a b c -> p (a b c)"),
                      start=True, stop=True).then_inc(rt_pe, 1)
            pe.matmul(PS[0:8, 7, 0:8], r8[:, 14, :], M("eye8", 8), start=True, stop=True).then_inc(rt_pe, 1)
            pe.wait_ge(rt, RT_WDT)
            for half in range(2):
                mm = pe.matmul(PS[64 * half:64 * half + 64, 7, 16:16 + PAIRS], M("b2", 8), wdT[:, PAIRS * half:PAIRS * half + PAIRS],
                               start=True, stop=True, skip_group_check=True)
            mm.then_inc(rt_pe, 1)

            def f0_hidden(n):
                p, k, half = n // 4, n // 2 % 2, n % 2
                b = PAIRS * half + p
                pe.wait_ge(sel_w1, 2 * (2 * p + half) + k + 1)
                pe.wait_ge(LN[1]["low"], chunks_for(p))
                pe.wait_ge(LN[1]["high"], chunks_for(p))
                if n < 2:
                    pe.wait_ge(LN[1]["normed"], 3)
                else:
                    pe.wait_ge(f0_act, n - 1)
                for j in range(2):
                    a = p * PIX + j * HALFPIX
                    for part in range(2):
                        mm = pe.matmul(PS[:, 2 * (n % 2) + j, 0:HALFPIX], w1sel[:, b, k, part, :], XS[:, half, a:a + HALFPIX],
                                       start=part == 0, stop=part == 1)
                mm.then_inc(f0_mm, 1)

            def f0_down(p, k):
                pe.wait_ge(f0_act, 4 * p + 2 * k + 2)
                pe.wait_ge(sel_w2, 2 * (2 * p + 1) + k + 1)
                if k == 0:
                    if p == 0:
                        pe.wait_ge(LN[1]["normed"], 1)
                    if p == 1:
                        pe.wait_ge(rt, RT_B2)
                    if p >= 2:
                        pe.wait_ge(f0_res, p - 1)
                for j in range(2):
                    for half in range(2):
                        mm = pe.matmul(PS[64 * half:64 * half + 64, 4 + 2 * (p % 2) + j, 0:HALFPIX], w2sel[:, PAIRS * half + p, k, :],
                                       h0[:, 2 * k + half, j * HALFPIX:(j + 1) * HALFPIX], start=k == 0, stop=k == 1,
                                       skip_group_check=True)
                mm.then_inc(f0_out, 1)

            f0_hidden(0)
            f0_hidden(1)
            for p in range(PAIRS):
                for k in range(2):
                    n = 4 * p + 2 * k + 2
                    if n < 4 * PAIRS:
                        f0_hidden(n)
                        f0_hidden(n + 1)
                    f0_down(p, k)

            layer_norm(2, lambda c: pe.wait_ge(f0_res, images_for(c)), lambda: pe.wait_ge(f0_act, 4 * PAIRS), nothing,
                       lambda: pe.wait_ge(f0_res, PAIRS - 1), lambda: pe.wait_ge(f0_res, PAIRS))
            layer_norm(3, lambda c: pe.wait_ge(x2_done, c + 1), lambda: pe.wait_ge(LN[2]["normed"], 3), nothing,
                       nothing, lambda: pe.wait_ge(LN[2]["rooted"], 3))

            pe.wait_ge(conv_w, 2)
            pe.wait_ge(LN[3]["normed"], 3)
            pe.wait_ge(LN[3]["rooted"], 3)
            for p in range(PAIRS):
                pe.wait_ge(LN[3]["high"], chunks_for(p))
                pe.wait_ge(LN[3]["low"], chunks_for(p))
                for half in range(2):
                    k = (2 * p + half) % 4
                    if p >= 2:
                        pe.wait_ge(conv_low, 2 * (p - 2) + half + 1)
                        pe.wait_ge(conv_a, 2 * (p - 2) + half + 1)
                    iv = img[:, PAIRS * half + p, :].rearrange("p (y z) -> p y z", z=PADW)
                    for j in range(2):
                        for tap in range(TAPS):
                            dy, dx = tap // 3, tap % 3
                            mm = pe.matmul(PS[:, 2 * k + j, 0:HALFPIX], conv_hl[:, tap, :, :].rearrange("p a o -> p (a o)"),
                                           iv[:, j * ROWS + dy:j * ROWS + dy + ROWS, dx:dx + WD],
                                           start=tap == 0, stop=tap == TAPS - 1)
                    mm.then_inc(conv_mm, 1)

            layer_norm(4, lambda c: pe.wait_ge(x3_done, images_for(c)),
                       lambda: (pe.wait_ge(conv_low, 2 * PAIRS), pe.wait_ge(conv_a, 2 * PAIRS)), nothing, nothing, nothing)

            pe.wait_ge(wg_s, 2)
            pe.wait_ge(LN[4]["rooted"], 3)
            for t in range(NT):
                pe.wait_ge(LN[4]["high"], t // TPC + 1)
                pe.wait_ge(LN[4]["low"], t // TPC + 1)
                for half in range(2):
                    n = 2 * t + half
                    for part in range(2):
                        mm = pe.matmul(PS[:, 6, EXP * n:EXP * n + EXP], XS[:, half, t * TILE:(t + 1) * TILE], wg_hl[:, part, :],
                                       start=part == 0, stop=part == 1)
            mm.then_inc(lg_mm, 1)

            pe.wait_ge(gt, GT_DONE)
            pe.wait_ge(LN[4]["normed"], 3)
            for c in range(NCH):
                for k in range(TPC):
                    t = TPC * c + k
                    mm = pe.matmul(PS[0:16, 2 * c + k // 3, (k % 3) * TILE:(k % 3 + 1) * TILE],
                                   gw[:, 2 * t:2 * t + 2, :].rearrange("p a e -> p (a e)"), E("ident"), start=True, stop=True)
                mm.then_inc(gT_mm, 1)

            pe.wait_ge(gT_lo, NCH)
            pe.wait_ge(gT_hi, NCH)
            pe.wait_ge(w1_hs, 1)
            pe.wait_ge(w1_ls, 1)
            pe.wait_ge(spread_s, 1)
            SLOTS = 5 * EXP

            for c in range(NCH):
                def ring_free(s):
                    n = SLOTS * c + s
                    if n >= 3:
                        pe.wait_ge(f1_act, n - 2)

                def gates(e):
                    s = 5 * e
                    ring_free(s)
                    k = (SLOTS * c + s) % 3
                    for j in range(2):
                        a = c * CHUNK + j * BANK
                        mm = pe.matmul(PS[:, 2 * k + j, 0:BANK], spread_r[:, e, :], gT[:, a:a + BANK], start=True, stop=True)
                    mm.then_inc(f1_mm, 1)

                def hidden(e, kk, half):
                    s = 5 * e + 1 + 2 * kk + half
                    ring_free(s)
                    k = (SLOTS * c + s) % 3
                    for j in range(2):
                        a = c * CHUNK + j * BANK
                        u = e * F1 + kk * 128
                        pe.matmul(PS[:, 2 * k + j, 0:BANK], w1_h[:, u:u + 128], XS[:, half, a:a + BANK], start=True, stop=False)
                        mm = pe.matmul(PS[:, 2 * k + j, 0:BANK], w1_l[:, u:u + 128], XS[:, half, a:a + BANK], start=False, stop=True)
                    mm.then_inc(f1_mm, 1)

                def down(e, kk):
                    pe.wait_ge(f1_act, SLOTS * c + 5 * e + 1 + 2 * kk + 2)
                    n = EXP * c + e
                    if kk == 0:
                        if n == 0:
                            pe.wait_ge(gt, 1)
                        else:
                            pe.wait_ge(o_mul, n)
                    u = (HID * e + kk) * CH
                    for j in range(2):
                        for half in range(2):
                            mm = pe.matmul(PS[64 * half:64 * half + 64, 6 + j, 0:BANK], L("w2")[:, u:u + CH],
                                           h1[:, 2 * kk + half, j * BANK:(j + 1) * BANK], start=kk == 0, stop=kk == HID - 1,
                                           skip_group_check=True)
                    mm.then_inc(f1_out, 1)

                gates(0)
                hidden(0, 0, 0)
                hidden(0, 0, 1)
                for e in range(EXP):
                    hidden(e, 1, 0)
                    hidden(e, 1, 1)
                    down(e, 0)
                    if e + 1 < EXP:
                        gates(e + 1)
                        hidden(e + 1, 0, 0)
                        hidden(e + 1, 0, 1)
                    down(e, 1)

        @block.scalar
        def _(act):
            def layer_norm(i, extra=None, highs=None):
                s = LN[i]
                e = 0 if i in (0, 3) else 1

                def square_copy(c):
                    act.wait_ge(s["centered"], c + 1)
                    if i > 0:
                        act.wait_ge(LN[i - 1]["summed"], 3)
                        act.wait_ge(LN[i - 1]["normed"], 3)
                    act.activation(cols(Q, c), pair(CEN[c]), ACT.Square).then_inc(s["squared"], 1)
                    act.activation(cols(D, c), pair(CEN[c]), ACT.Copy).then_inc(s["copied"], 1)

                def root(c):
                    act.wait_ge(s["summed"], c + 1)
                    if i > 0:
                        act.wait_ge(LN[i - 1]["inverted"], 3)
                    t = 2 * TPC * c
                    act.activation(dev[:, t:t + 2 * TPC], PS[:, SUM[c], t:t + 2 * TPC], ACT.Sqrt,
                                   bias=eps[:, e:e + 1]).then_inc(s["rooted"], 1)

                def high(c):
                    act.wait_ge(s["normed"], c + 1)
                    highs(c).then_inc(s["high"], 1)

                square_copy(0)
                square_copy(1)
                root(0)
                square_copy(2)
                root(1)
                if highs:
                    high(0)
                root(2)
                if highs:
                    high(1)
                    high(2)

            def high_parts(c):
                a = c * CHUNK
                act.activation(XS[0:64, 0, a:a + CHUNK], N[0:64, a:a + CHUNK], ACT.Copy)
                return act.activation(XS[64:128, 1, a:a + CHUNK], N[64:128, a:a + CHUNK], ACT.Copy)

            act.wait_ge(early_ld, 16)
            act.activation(perm_r[:, :, :].rearrange("p t m -> p (t m)"), E("perm"), ACT.Copy).then_inc(prep_r, 1)
            act.activation(l1sum_r[:, :], E("l1sum"), ACT.Copy).then_inc(prep_r, 1)
            act.wait_ge(epsset, 1)
            act.activation(bnw[:, 0:1], E("bn1")[:, 3:4], ACT.Sqrt, bias=eps[:, 1:2]).then_inc(bn_a, 1)
            act.activation(bnw[:, 4:5], E("bn2")[:, 3:4], ACT.Sqrt, bias=eps[:, 1:2]).then_inc(bn_a, 1)

            layer_norm(0, highs=high_parts)

            act.wait_ge(fold, 2)
            for c in range(NCH):
                for half in range(2):
                    n = 2 * c + half
                    act.wait_ge(amp_mm, n + 1)
                    act.activation(cols(amp[:, half], c), pair(n % 2), ACT.Relu, bias=bnw[:, 3:4], scale=bnw[:, 2:3]).then_inc(amp_done, 1)

            def y_relu(c):
                act.wait_ge(y_scaled, c + 1)
                act.activation(cols(yraw, c), cols(yraw, c), ACT.Relu, bias=bnw[:, 7:8], scale=bnw[:, 6:7]).then_inc(y_act, 1)

            for c in range(NCH):
                act.wait_ge(y_mm, GT * (c + 1))
                act.activation(cols(yraw, c), pair(2), ACT.Copy).then_inc(y_copied, 1)
                if c > 0:
                    y_relu(c - 1)
            y_relu(NCH - 1)

            act.wait_ge(amp_mm, 2 * NCH)
            layer_norm(1, highs=high_parts)

            act.wait_ge(rt, RT_L1)
            act.activation(r8[:, 3, :], r8[:, 0, :], ACT.Exp, bias=r8[:, 1, 0:1], accum_out=r8[:, 2, 0:1]).then_inc(rt_act, 1)
            act.wait_ge(rt, RT_L2)
            act.activation(r8[:, 7, :], r8[:, 5, :], ACT.Exp, bias=r8[:, 6, 0:1], accum_out=r8[:, 2, 1:2]).then_inc(rt_act, 1)
            act.wait_ge(rt, RT_DIFF)
            act.activation(r8[:, 12, 1:2], r8[:, 12, 0:1], ACT.Exp).then_inc(rt_act, 1)

            def f0_gelu(n):
                p, k, half = n // 4, n // 2 % 2, n % 2
                b = PAIRS * half + p
                act.wait_ge(f0_mm, n + 1)
                act.wait_ge(sel_b1, 2 * (2 * p + half) + k + 1)
                if n >= 4:
                    act.wait_ge(f0_out, 2 * (p - 1) + k + 1)
                act.activation(h0[:, 2 * k + half, :].rearrange("p (j n) -> p j n", j=2), pair(n % 2, HALFPIX), ACT.Gelu,
                               bias=b1sel[:, b, k:k + 1]).then_inc(f0_act, 1)

            for n in range(4 * PAIRS):
                f0_gelu(n)

            layer_norm(2)

            def image_high(c):
                last = None
                for lo, p, y0, ny in pieces(c):
                    a = p * PIX + y0 * WD
                    for half in range(2):
                        q = slice(64 * half, 64 * half + 64)
                        iv = img[q, PAIRS * half + p, :].rearrange("p (y z) -> p y z", z=PADW)
                        last = act.activation(iv[:, 1 + y0:1 + y0 + ny, 1:1 + WD],
                                              N[q, a:a + ny * WD].rearrange("p (y z) -> p y z", z=WD), ACT.Copy)
                return last

            act.wait_ge(img0, 1)
            layer_norm(3, highs=image_high)

            for n in range(2 * PAIRS):
                p, half = n // 2, n % 2
                act.wait_ge(conv_mm, n + 1)
                src = pair(n % 4, HALFPIX, 64 - 64 * half, 128 - 64 * half)
                act.activation(icols(clow, p, 64 * half, 64 * half + 64), src, ACT.Copy, scale=1.0 / TAPS).then_inc(conv_low, 1)

            act.wait_ge(f0_mm, 4 * PAIRS)
            layer_norm(4, highs=high_parts)

            act.wait_ge(gt, GT_EXP)
            act.activation(gw[:, :, :], gcmp[:, :, :], ACT.Exp).then_inc(gt_act, 1)

            act.wait_ge(late_ld, 16)
            SLOTS = 5 * EXP

            def ring(c, e, s):
                n = SLOTS * c + 5 * e + s
                act.wait_ge(f1_mm, n + 1)
                if s == 0:
                    if EXP * c + e >= 2:
                        act.wait_ge(o_mul, EXP * c + e - 1)
                    act.activation(gB[:, e % 2, :].rearrange("p (j n) -> p j n", j=2), pair(n % 3), ACT.Copy).then_inc(f1_act, 1)
                else:
                    kk, half = (s - 1) // 2, (s - 1) % 2
                    if EXP * c + e >= 1:
                        act.wait_ge(f1_out, HID * (EXP * c + e - 1) + kk + 1)
                    act.activation(h1[:, 2 * kk + half, :].rearrange("p (j n) -> p j n", j=2), pair(n % 3), ACT.Gelu,
                                   bias=L("b1")[:, HID * e + kk:HID * e + kk + 1]).then_inc(f1_act, 1)

            for c in range(NCH):
                for e in range(EXP):
                    for s in range(5):
                        ring(c, e, s)

        @block.vector
        def _(ve):
            def layer_norm(i, normalize, lows=None):
                s = LN[i]

                def invert(c):
                    ve.wait_ge(s["rooted"], c + 1)
                    if i > 0:
                        ve.wait_ge(LN[i - 1]["spread"], 3)
                    t = 2 * TPC * c
                    ve.reciprocal(rdev[:, t:t + 2 * TPC], dev[:, t:t + 2 * TPC]).then_inc(s["inverted"], 1)

                def norm(c):
                    ve.wait_ge(s["spread"], c + 1)
                    ve.wait_ge(s["copied"], c + 1)
                    normalize(c)

                def low(c):
                    ve.wait_ge(s["high"], c + 1)
                    ve.wait_ge(s["normed"], c + 1)
                    lows(c).then_inc(s["low"], 1)

                invert(0)
                invert(1)
                norm(0)
                invert(2)
                norm(1)
                if lows:
                    low(0)
                norm(2)
                if lows:
                    low(1)
                    low(2)

            def plain(i):
                def normalize(c):
                    ve.tensor_tensor(cols(N, c), pair(BC[c]), cols(D, c), ALU.mult).then_inc(LN[i]["normed"], 1)
                return normalize

            def low_parts(c):
                a = c * CHUNK
                ve.tensor_tensor(XS[64:128, 0, a:a + CHUNK], N[0:64, a:a + CHUNK], XS[0:64, 0, a:a + CHUNK].bitcast(F32), ALU.subtract)
                return ve.tensor_tensor(XS[0:64, 1, a:a + CHUNK], N[64:128, a:a + CHUNK],
                                        XS[64:128, 1, a:a + CHUNK].bitcast(F32), ALU.subtract)

            ve.memset(eps[:, 0:1], 1e-6)
            ve.memset(eps[:, 1:2], 1e-5).then_inc(epsset, 1)
            ve.memset(img[:, :, :].bitcast(F32).rearrange("p b n -> p (b n)"), 0.0).then_inc(img0, 1)
            ve.memset(msum[:, :], 0.0).then_inc(msum0, 1)

            ve.wait_ge(early_ld, 16)
            ve.tensor_copy(w11_hl[:, 0, :], E("w11")).then_inc(prep_w11, 1)
            ve.wait_ge(prep_w11, 1)
            ve.tensor_tensor(w11_hl[:, 1, :], E("w11"), w11_hl[:, 0, :].bitcast(F32), ALU.subtract).then_inc(prep_w11, 1)
            ve.wait_ge(bn_a, 2)
            for k, name in enumerate(("bn1", "bn2")):
                g, b, m = (E(name)[:, q:q + 1] for q in range(3))
                o = 4 * k
                ve.reciprocal(bnw[:, o + 1:o + 2], bnw[:, o:o + 1]).then_inc(bn_b, 1)
                ve.wait_ge(bn_b, 4 * k + 1)
                ve.tensor_tensor(bnw[:, o + 2:o + 3], bnw[:, o + 1:o + 2], g, ALU.mult).then_inc(bn_b, 1)
                ve.wait_ge(bn_b, 4 * k + 2)
                ve.tensor_tensor(bnw[:, o + 1:o + 2], bnw[:, o + 2:o + 3], m, ALU.mult).then_inc(bn_b, 1)
                ve.wait_ge(bn_b, 4 * k + 3)
                ve.tensor_tensor(bnw[:, o + 3:o + 4], b, bnw[:, o + 1:o + 2], ALU.subtract).then_inc(bn_b, 1)
                ve.wait_ge(bn_b, 4 * k + 4)
                ve.tensor_copy(bnw[:, o:o + 1], bnw[:, o + 3:o + 4]).then_inc(fold, 1)

            layer_norm(0, plain(0), low_parts)

            for c in range(NCH):
                for half in range(2):
                    n = 2 * c + half
                    a = c * CHUNK
                    ve.wait_ge(amp_done, n + 1)
                    ve.tensor_copy(amp_s[:, half, a:a + CHUNK], amp[:, half, a:a + CHUNK]).then_inc(amp_hi, 1)
                    ve.wait_ge(amp_hi, n + 1)
                    low = amp_s[64:128, half, a:a + CHUNK]
                    ve.tensor_tensor(low, amp[64:128, half, a:a + CHUNK], low.bitcast(F32), ALU.subtract).then_inc(amp_lo, 1)

            for c in range(NCH):
                t = 2 * TPC * c
                r = slice(t, t + 2 * TPC)
                ve.wait_ge(l1_mm, c + 1)
                src = PS[:, SUM[c], 2 * t:2 * t + 4 * TPC].rearrange("p (n two) -> p n two", two=2)[:, :, 0]
                ve.tensor_scalar(rl1[:, r], src, 1e-12, None, ALU.max).then_inc(l1_max, 1)
                ve.wait_ge(l1_max, c + 1)
                ve.reciprocal(rl1sq[:, r], rl1[:, r]).then_inc(l1_inv, 1)
                ve.wait_ge(l1_inv, c + 1)
                ve.tensor_tensor(rl1sq[:, r], rl1sq[:, r], rl1sq[:, r], ALU.mult).then_inc(l1_sq, 1)

            def scale_y(c):
                ve.wait_ge(y_copied, c + 1)
                ve.wait_ge(l1_bc, c + 1)
                ve.tensor_tensor(cols(yraw, c), pair(3), cols(yraw, c), ALU.mult).then_inc(y_scaled, 1)

            for n in range(8 * NCH):
                c, t, half = n // 8, n // 2 % 4, n % 2
                ve.wait_ge(shift_mm, n + 1)
                if n >= 4:
                    ve.wait_ge(y_mm, n // 2 - 1)
                ve.tensor_tensor(gram[:, 2 * (t % 2) + half, :].rearrange("p (j n) -> p j n", j=2), pair(n % 2),
                                 cols(amp[:, half], c), ALU.mult).then_inc(gram_done, 1)
                if n % 8 == 3 and c > 0:
                    scale_y(c - 1)
            scale_y(NCH - 1)
            for c in range(NCH):
                ve.wait_ge(fc_mm, c + 1)
                ve.scalar_tensor_tensor(out=cols(X, c), in0=pair(c % 2), scalar=E("bfc"), in1=cols(X, c),
                                        op0=ALU.add, op1=ALU.add).then_inc(x1_done, 1)

            layer_norm(1, plain(1), low_parts)

            ve.wait_ge(mix0_ld, 16)
            ve.tensor_copy(w1m_hl[:, :, 0, :], M("w1").rearrange("p (e f) -> p e f", e=EXP)).then_inc(m0_hi, 1)
            ve.wait_ge(m0_hi, 1)
            ve.tensor_tensor(w1m_hl[:, :, 1, :], M("w1").rearrange("p (e f) -> p e f", e=EXP),
                             w1m_hl[:, :, 0, :].bitcast(F32), ALU.subtract).then_inc(m0_lo, 1)

            step = [0]

            def then(ins):
                ins.then_inc(rt, 1)
                step[0] += 1
                ve.wait_ge(rt, step[0])
                return step[0]

            ve.wait_ge(msum0, 1)
            then(ve.tensor_reduce(imsum[:, :], N[:, :].rearrange("p (b n) -> p b n", b=PAIRS), AX, ALU.add))
            then(ve.tensor_copy(msum[0:64, 0:PAIRS], imsum[0:64, :]))
            then(ve.tensor_copy(msum[64:128, PAIRS:BATCH], imsum[64:128, :]))
            ve.wait_ge(rt_pe, 1)
            then(ve.scalar_tensor_tensor(out=r8[:, 0, :], in0=PS[0:8, 6, 0:8], scalar=1.0 / PIX, in1=M("br", 8),
                                         op0=ALU.mult, op1=ALU.add))
            then(ve.tensor_reduce(r8[:, 1, 0:1], r8[:, 0, :], AX, ALU.max, negate=True))
            assert step[0] == RT_L1
            ve.wait_ge(rt_act, 1)
            then(ve.reciprocal(r8[:, 1, 1:2], r8[:, 2, 0:1]))
            then(ve.tensor_scalar(r8[:, 4, :], r8[:, 3, :], r8[:, 1, 1:2], None, ALU.mult))
            assert step[0] == RT_SOFT1
            ve.wait_ge(rt_pe, 2)
            then(ve.reciprocal(r8[:, 10, :], PS[0:8, 6, 8:16]))
            then(ve.tensor_scalar(r8[:, 10, :], r8[:, 10, :], CAPACITY / PIX, 1.0, ALU.mult, ALU.min))
            then(ve.tensor_tensor(r8[:, 5, :], r8[:, 4, :], r8[:, 10, :], ALU.mult))
            then(ve.tensor_reduce(r8[:, 6, 0:1], r8[:, 5, :], AX, ALU.max, negate=True))
            assert step[0] == RT_L2
            ve.wait_ge(rt_act, 2)
            then(ve.reciprocal(r8[:, 1, 2:3], r8[:, 2, 1:2]))
            then(ve.tensor_scalar(r8[:, 8, :], r8[:, 7, :], r8[:, 1, 2:3], None, ALU.mult))
            cmp3 = [r88[:, q, :].rearrange("p (e f) -> p e f", e=EXP) for q in range(4)]
            mine = r8[:, 8, :].unsqueeze(2).to_broadcast([8, EXP, EXP])
            others = r8[:, 8, :].unsqueeze(1).to_broadcast([8, EXP, EXP])
            then(ve.tensor_tensor(cmp3[0], others, mine, ALU.is_gt))
            then(ve.tensor_tensor(cmp3[1], others, mine, ALU.is_ge))
            then(ve.tensor_tensor(r88[:, 0, :], r88[:, 0, :], M("above", 8), ALU.mult))
            then(ve.tensor_tensor(r88[:, 1, :], r88[:, 1, :], M("below", 8), ALU.mult))
            then(ve.tensor_tensor(r88[:, 2, :], r88[:, 0, :], r88[:, 1, :], ALU.add))
            then(ve.tensor_reduce(r8[:, 9, :], cmp3[2], AX, ALU.add))
            for k in range(2):
                then(ve.tensor_scalar(pick[:, k, :], r8[:, 9, :], float(k), None, ALU.is_equal))
                then(ve.tensor_tensor(r8[:, 11, :], pick[:, k, :], M("iota", 8), ALU.mult))
                then(ve.tensor_reduce(pickv[:, k:k + 1], r8[:, 11, :], AX, ALU.add))
                then(ve.tensor_tensor(r8[:, 11, :], pick[:, k, :], r8[:, 8, :], ALU.mult))
                then(ve.tensor_reduce(r8[:, 13, k:k + 1], r8[:, 11, :], AX, ALU.add))
            then(ve.tensor_tensor(r8[:, 12, 0:1], r8[:, 13, 1:2], r8[:, 13, 0:1], ALU.subtract))
            assert step[0] == RT_DIFF
            ve.wait_ge(rt_act, 3)
            then(ve.tensor_scalar(r8[:, 12, 2:3], r8[:, 12, 1:2], 1.0, None, ALU.add))
            then(ve.reciprocal(pickv[:, 2:3], r8[:, 12, 2:3]))
            then(ve.tensor_tensor(pickv[:, 3:4], r8[:, 12, 1:2], pickv[:, 2:3], ALU.mult))
            then(ve.tensor_scalar(r8[:, 15, :], pick[:, 0, :], pickv[:, 2:3], None, ALU.mult))
            then(ve.scalar_tensor_tensor(out=r8[:, 14, :], in0=pick[:, 1, :], scalar=pickv[:, 3:4], in1=r8[:, 15, :],
                                         op0=ALU.mult, op1=ALU.add))
            diag = M("diag", 8).rearrange("p (b k) -> p b k", b=BATCH)
            for q in range(2):
                val = pickv[:, 2 * q:2 * q + 2].unsqueeze(1).to_broadcast([8, BATCH, 2])
                then(ve.tensor_tensor(pickd[:, q, :, :], diag, val, ALU.mult))
            assert step[0] == RT_PICKED
            ve.wait_ge(rt_pe, 3)
            then(ve.tensor_copy(pickb[:, :], PS[:, 6, 16:48]))
            then(ve.tensor_copy(picki[:, :], PS[0:1, 6, 16:32]))
            assert step[0] == RT_IDX
            ve.wait_ge(rt_pe, 4)
            then(ve.tensor_copy(wdT[:, :], PS[0:8, 7, 0:8]))
            assert step[0] == RT_WDT
            ve.wait_ge(rt_pe, 5)
            then(ve.tensor_copy(b2sel[:, :], PS[:, 7, 16:16 + PAIRS]))
            assert step[0] == RT_B2

            ve.wait_ge(m0_lo, 1)
            w2b1 = M("w2b1").rearrange("p (e n) -> p e n", e=EXP)
            for p in range(PAIRS):
                for half in range(2):
                    b = PAIRS * half + p
                    for k in range(2):
                        e = ve.value_load(picki[0:1, 2 * b + k:2 * b + k + 1], min_val=0, max_val=EXP - 1)
                        ve.tensor_copy(w1sel[:, b, k, :, :], w1m_hl[:, bass.ds(e, 1), :, :].bitcast(F32)).then_inc(sel_w1, 1)
                        wk = pickb[:, 16 + 2 * b + k:16 + 2 * b + k + 1]
                        ve.tensor_scalar(w2sel[:, b, k, :], w2b1[:, bass.ds(e, 1), 0:CH], wk, None, ALU.mult).then_inc(sel_w2, 1)
                        ve.tensor_copy(b1sel[:, b, k:k + 1], w2b1[:, bass.ds(e, 1), CH:CH + 1]).then_inc(sel_b1, 1)

            ve.tensor_scalar(clow[:, :], X[:, :], M("beta"), None, ALU.add).then_inc(xbeta, 1)
            ve.wait_ge(xbeta, 1)
            for p in range(PAIRS):
                ve.wait_ge(f0_out, 2 * p + 2)
                ve.scalar_tensor_tensor(out=icols(X, p), in0=pair(2 + p % 2, HALFPIX), scalar=b2sel[:, p:p + 1],
                                        in1=icols(N, p), op0=ALU.add, op1=ALU.add).then_inc(f0_res, 1)

            def affine(c):
                ve.scalar_tensor_tensor(out=cols(N, c), in0=pair(BC[c]), scalar=M("gamma"), in1=cols(D, c),
                                        op0=ALU.mult, op1=ALU.mult).then_inc(LN[2]["normed"], 1)
                ve.wait_ge(LN[2]["normed"], c + 1)
                ve.wait_ge(LN[2]["centered"], 3)
                ve.tensor_tensor(cols(X, c), cols(N, c), cols(clow, c), ALU.add).then_inc(x2_done, 1)

            layer_norm(2, affine)

            def image_low(c):
                last = None
                for lo, p, y0, ny in pieces(c):
                    a = p * PIX + y0 * WD
                    for half in range(2):
                        q = slice(64 * half, 64 * half + 64)
                        o = slice(64 - 64 * half, 128 - 64 * half)
                        hv = img[q, PAIRS * half + p, :].rearrange("p (y z) -> p y z", z=PADW)
                        lv = img[o, PAIRS * half + p, :].rearrange("p (y z) -> p y z", z=PADW)
                        last = ve.tensor_tensor(lv[:, 1 + y0:1 + y0 + ny, 1:1 + WD],
                                                N[q, a:a + ny * WD].rearrange("p (y z) -> p y z", z=WD),
                                                hv[:, 1 + y0:1 + y0 + ny, 1:1 + WD].bitcast(F32), ALU.subtract)
                return last

            ve.wait_ge(img0, 1)
            ve.wait_ge(late_ld, 16)
            cw = L("conv").rearrange("p (t o) -> p t o", t=TAPS)
            ve.tensor_copy(conv_hl[:, :, 0, :], cw).then_inc(conv_w, 1)
            ve.wait_ge(conv_w, 1)
            ve.tensor_tensor(conv_hl[:, :, 1, :], cw, conv_hl[:, :, 0, :].bitcast(F32), ALU.subtract).then_inc(conv_w, 1)

            layer_norm(3, plain(3), image_low)

            for p in range(PAIRS):
                for half in range(2):
                    n = 2 * p + half
                    q = (64 * half, 64 * half + 64)
                    ve.wait_ge(conv_low, n + 1)
                    ve.scalar_tensor_tensor(out=icols(clow, p, *q), in0=pair(n % 4, HALFPIX, *q), scalar=1.0 / TAPS,
                                            in1=icols(clow, p, *q), op0=ALU.mult, op1=ALU.add).then_inc(conv_a, 1)
                ve.wait_ge(conv_a, 2 * p + 2)
                ve.tensor_tensor(icols(X, p), icols(X, p), icols(clow, p), ALU.add).then_inc(x3_done, 1)

            ve.tensor_copy(wg_hl[:, 0, :], L("wg")).then_inc(wg_s, 1)
            ve.wait_ge(wg_s, 1)
            ve.tensor_tensor(wg_hl[:, 1, :], L("wg"), wg_hl[:, 0, :].bitcast(F32), ALU.subtract).then_inc(wg_s, 1)

            layer_norm(4, plain(4), low_parts)

            ve.wait_ge(lg_mm, 1)
            g = [0]

            def gthen(ins):
                ins.then_inc(gt, 1)
                g[0] += 1
                ve.wait_ge(gt, g[0])

            NG = NT * 2
            gthen(ve.tensor_tensor(lg[:, :, :], PS[:, 6, 0:NG * EXP].rearrange("p (n e) -> p n e", e=EXP),
                                   L("bg").unsqueeze(1).to_broadcast([128, NG, EXP]), ALU.add))
            gthen(ve.tensor_reduce(gmx[:, 0, :], lg[:, :, :], AX, ALU.max))
            gthen(ve.tensor_tensor(gcmp[:, :, :], lg[:, :, :], gmx[:, 0, :].unsqueeze(2).to_broadcast([128, NG, EXP]), ALU.subtract))
            assert g[0] == GT_EXP
            gthen(ve.memset(rank[:, :, 0:1], 0.0))
            for e in range(1, EXP):
                gthen(ve.memset(rank[:, :, e:e + 1], float(e)))
            ve.wait_ge(gt_act, 1)
            for s in range(1, EXP):
                n = EXP - s
                gthen(ve.tensor_tensor(gcmp[:, :, 0:n], lg[:, :, s:EXP], lg[:, :, 0:n], ALU.is_gt))
                gthen(ve.tensor_tensor(rank[:, :, 0:n], rank[:, :, 0:n], gcmp[:, :, 0:n], ALU.add))
                gthen(ve.tensor_tensor(rank[:, :, s:EXP], rank[:, :, s:EXP], gcmp[:, :, 0:n], ALU.subtract))
            gthen(ve.tensor_scalar(rank[:, :, :], rank[:, :, :], 2.0, None, ALU.is_lt))
            gthen(ve.tensor_tensor(gw[:, :, :], gw[:, :, :], rank[:, :, :], ALU.mult))
            gthen(ve.tensor_reduce(gmx[:, 1, :], gw[:, :, :], AX, ALU.add))
            gthen(ve.reciprocal(gmx[:, 2, :], gmx[:, 1, :]))
            gthen(ve.tensor_tensor(gw[:, :, :], gw[:, :, :], gmx[:, 2, :].unsqueeze(2).to_broadcast([128, NG, EXP]), ALU.mult))
            assert g[0] == GT_DONE

            ve.tensor_copy(w1_h[:, :], L("w1")).then_inc(w1_hs, 1)
            ve.wait_ge(w1_hs, 1)
            ve.tensor_tensor(w1_l[:, :], L("w1"), w1_h[:, :].bitcast(F32), ALU.subtract).then_inc(w1_ls, 1)
            ve.tensor_copy(spread_r[:, :, :].rearrange("p e m -> p (e m)"), L("spread", 48)).then_inc(spread_s, 1)

            ve.memset(gT[0:32, :].bitcast(F32), 0.0).then_inc(gT0, 1)
            ve.wait_ge(gT0, 1)
            for c in range(NCH):
                ve.wait_ge(gT_mm, c + 1)
                ve.tensor_copy(cols(gT, c, 0, 16), pair(c, BANK, 0, 16)).then_inc(gT_hi, 1)
                ve.wait_ge(gT_hi, c + 1)
                ve.tensor_tensor(cols(gT, c, 32, 48), pair(c, BANK, 0, 16), cols(gT, c, 0, 16).bitcast(F32), ALU.subtract).then_inc(gT_lo, 1)

            for c in range(NCH):
                for e in range(EXP):
                    n = EXP * c + e
                    ve.wait_ge(f1_out, HID * n + HID)
                    ve.wait_ge(f1_act, 5 * n + 1)
                    gv = gB[:, e % 2, :].rearrange("p (j n) -> p j n", j=2)
                    tv = tmp[:, :].rearrange("p (j n) -> p j n", j=2)
                    if n:
                        ve.wait_ge(o_add, n)
                    ve.scalar_tensor_tensor(out=tv, in0=pair(3), scalar=L("b2")[:, e:e + 1], in1=gv,
                                            op0=ALU.add, op1=ALU.mult).then_inc(o_mul, 1)
                    ve.wait_ge(o_mul, n + 1)
                    ve.tensor_tensor(cols(X, c), tv, cols(X, c), ALU.add).then_inc(o_add, 1)




def halves(a):
    return np.concatenate([a, a], axis=0)


def column(v):
    return np.reshape(v, (-1, 1))


def blockdiag(a):
    out = np.zeros((128, 128), np.float32)
    out[0:64, 0:64] = a
    out[64:128, 64:128] = a
    return out


def pack(table, parts):
    at, n = places(table)
    out = np.zeros((128, n), np.float32)
    for name, (a, b) in at.items():
        part = np.asarray(parts[name])
        part = part.reshape(part.shape[0], -1)
        out[0:part.shape[0], a:b] = part
    return out


def shift_of(t, s):
    return GT * t + s + 1


def gram_weights(w12):
    first, second = np.triu_indices(MID, k=1)
    number = np.zeros((MID, MID), np.int64)
    number[first, second] = np.arange(len(first))
    out = np.zeros((128, GT, CH), np.float32)
    for t in range(GT):
        for s in range(4):
            d = shift_of(t, s)
            for i in range(MID if d < MID // 2 else MID // 2):
                j = (i + d) % MID
                out[MID * s + i, t] = w12[:, number[min(i, j), max(i, j)]]
    return out


def shift_matrices():
    out = np.zeros((128, GT, 128), np.float32)
    for t in range(GT):
        for s in range(4):
            for i in range(MID):
                j = (i + shift_of(t, s)) % MID
                out[j, t, MID * s + i] = 1
                out[64 + j, t, MID * s + i] = 1
    return out


def spread_matrices():
    out = np.zeros((48, EXP, 128), np.float32)
    for e in range(EXP):
        for half in range(2):
            for part in range(2):
                out[32 * part + EXP * half + e, e, 64 * half:64 * half + 64] = 1
    return out


def packed(v):
    blockmean = np.zeros((128, 2), np.float32)
    blockmean[0:64, 0] = 1 / CH
    blockmean[64:128, 1] = 1 / CH
    diag = np.zeros((8, BATCH, 2), np.float32)
    diag[np.arange(8), np.arange(8)] = 1
    lower = np.tril(np.ones((EXP, EXP), np.float32), -1)
    early = pack(EARLY, {
        "center": blockdiag(np.eye(CH, dtype=np.float32) - np.float32(1 / CH)),
        "blockmean": blockmean,
        "ident": np.eye(128, dtype=np.float32),
        "w11": halves(np.concatenate([v["L0_conv_w11"].T] * 4, axis=1)),
        "bn1": np.concatenate([np.stack([v[f"L0_conv_{q}1"] for q in "gbmv"], axis=1)] * 4, axis=0),
        "bn2": halves(np.stack([v[f"L0_conv_{q}2"] for q in "gbmv"], axis=1)),
        "bfc": halves(column(v["L0_conv_bfc"])),
        "l1sum": np.full((128, 2), 0.5, np.float32),
        "perm": shift_matrices(),
        "w12": gram_weights(v["L0_conv_w12"]),
        "wfcy": blockdiag(v["L0_conv_wfc"][:, 0:CH].T),
        "wfcx": blockdiag(v["L0_conv_wfc"][:, CH:2 * CH].T),
    })
    mix0 = pack(MIX0, {
        "wr": halves(v["L0_ffn_Wr"]),
        "br": np.stack([v["L0_ffn_br"]] * 8),
        "below": np.stack([lower] * 8),
        "above": np.stack([lower.T] * 8),
        "iota": np.stack([np.arange(EXP, dtype=np.float32)] * 8),
        "eye8": np.eye(8, dtype=np.float32),
        "diag": diag,
        "ones8": np.ones((8, 128), np.float32),
        "b2": v["L0_ffn_b2"],
        "gamma": halves(column(v["L0_ffn_gamma"])),
        "beta": halves(column(v["L0_ffn_beta"])),
        "w1": halves(v["L0_ffn_W1"].transpose(1, 0, 2)),
        "w2b1": np.concatenate([v["L0_ffn_W2"].transpose(1, 0, 2), v["L0_ffn_b1"].T[:, :, None]], axis=2),
    })
    late = pack(LATE, {
        "conv": halves(v["L1_conv_w"].reshape(CH, CH, TAPS).transpose(1, 2, 0)),
        "wg": halves(v["L1_ffn_Wg"]),
        "bg": np.stack([v["L1_ffn_bg"]] * 128),
        "spread": spread_matrices(),
        "b1": v["L1_ffn_b1"].reshape(UNITS, 128).T,
        "b2": halves(v["L1_ffn_b2"].T),
        "w1": halves(v["L1_ffn_W1"].transpose(1, 0, 2)),
        "w2": v["L1_ffn_W2"].reshape(UNITS, 128, CH).transpose(1, 0, 2),
    })
    return early, mix0, late


def kernel(**inputs):
    import concourse.bacc as bacc
    from concourse.bass_utils import run_bass_kernel_spmd

    v = {name: np.asarray(a) for name, a in inputs.items()}
    early, mix0, late = packed(v)
    arrays = {"x_in": np.ascontiguousarray(v["x"]), "early_in": early, "mix0_in": mix0, "late_in": late}
    nc = bacc.Bacc("TRN2", target_bir_lowering=False, num_devices=1)
    aps = [nc.dram_tensor(name, a.shape, F32, kind="ExternalInput").ap() for name, a in arrays.items()]
    out = nc.dram_tensor("out", (BATCH, CH, HT, WD), F32, kind="ExternalOutput").ap()
    build(nc, *aps, out)
    return run_bass_kernel_spmd(nc, [arrays], core_ids=[0]).results[0]["out"]
```

```python
from contextlib import ExitStack

import numpy as np

import concourse.bass as bass
from concourse import mybir

BATCH, CH, HT, WD = 8, 64, 24, 24
PIX = HT * WD
MID = 32
EXP = 8
F0 = 128
F1 = 256
HID = F1 // 128
PAIRS = BATCH // 2
COLS = PAIRS * PIX
BANK = 384
TILE = 128
NT = COLS // TILE
NCH = COLS // BANK
CT = BANK // TILE
GROUPS = 2
GCH = NCH // GROUPS
GCOLS = COLS // GROUPS
GTILES = NT // GROUPS
GN = 2 * GTILES
HALFPIX = PIX // 2
ROWS = HT // 2
GT = 4
TAPS = 9
PADW = WD + 2
PADN = (HT + 2) * PADW
CAPACITY = -(-BATCH * PIX * 5 // (4 * EXP))
UNITS = EXP * HID

F32 = mybir.dt.float32
F32R = mybir.dt.float32r
I32 = mybir.dt.int32
ALU = mybir.AluOpType
ACT = mybir.ActivationFunctionType
AX = mybir.AxisListType.X

EARLY = {
    "center": 128, "blockmean": 2, "ident": 128, "w11": 128, "bn1": 4, "bn2": 4, "bfc": 1,
    "l1sum": 2, "perm": GT * 128, "w12": GT * CH, "wfcy": 128, "wfcx": 128,
}
MIX0 = {
    "wr": EXP, "br": EXP, "order": EXP, "eye8": 8, "diag": 16,
    "ones8": 128, "b2": CH, "gamma": 1, "beta": 1, "w1": EXP * F0, "w2b1": EXP * (CH + 1),
}
LATE = {
    "conv": TAPS * CH, "wg": EXP, "bg": EXP, "order": EXP, "spread": EXP * 128, "b1": UNITS, "b2": EXP,
    "w1": EXP * F1, "w2": UNITS * CH,
}


def places(table):
    out, at = {}, 0
    for name, n in table.items():
        out[name] = (at, at + n)
        at += n
    return out, at


def chunk(c):
    return slice(c * BANK, (c + 1) * BANK)


def tiles(c):
    return range(CT * c, CT * (c + 1))


def chunks_for(p):
    return -(-(p + 1) * PIX // BANK)


def images_for(c):
    return -(-(c + 1) * BANK // PIX)


def images_in(c):
    return c * BANK // PIX


def pieces(c):
    out, a = [], c * BANK
    while a < (c + 1) * BANK:
        p, y0 = a // PIX, a % PIX // WD
        ny = min(HT - y0, ((c + 1) * BANK - a) // WD)
        out.append((p, y0, ny))
        a += ny * WD
    return out


RT_SUM, RT_L1, RT_SOFT1, RT_L2, RT_DIFF, RT_PICKED, RT_IDX, RT_WDT, RT_B2 = 1, 3, 5, 9, 18, 29, 31, 32, 33
GT_LOGITS, GT_EXP, GT_ALL = 2, 4, 18
GATE_PIECES = 4
FAR = 3e38
UNITS_OF_RING = 5 * EXP
RING2_EXPERTS = 8
RING2 = 5 * RING2_EXPERTS

LN_BANK = [[6, 7, 5, 6, 6, 6], [7, 7, 7, 7, 7, 6]]
SHIFT_BANK = [0, 1, 3]
GROUP_BANK = [0, 6]
CONV_PAIR = [1, 2, 1, 2, 3, 3, 3, 3]
LOGIT_BANK = [3, 6]
TURN_BANK = [[4, 5, 4], [7, 6, 7]]


def ln_bank(i, c):
    return LN_BANK[i][c] if i < 2 else GROUP_BANK[c // GCH] + (c % GCH + i) % 2


STAGE1 = {
    ("center", 0): -35,
    ("sums", 0): -30.5,
    ("spread", 0): -29,
    ("parts", 0): -25.5,
    ("amplify", 0): -15,
    ("amplify", 1): -13,
    ("l1",): -11,
    ("spread_l1",): 7.5,
    ("fc",): 10.5,
    ("center", 1): 13.5,
    ("sums", 1): 17,
    ("spread", 1): 18.5,
    ("parts", 1): 21.5,
}
FIRST = {
    ("center", 0): -35.5,
    ("sums", 0): -35,
    ("spread", 0): -23,
    ("parts", 0): -21.5,
    ("amplify", 0): -15,
    ("amplify", 1): -13,
    ("l1",): -11.5,
}
CONSTANTS_AT = -26.5
SHIFTED_AT = -3.5
SHIFTED_STEP = 1.5


def first_stages():
    out = [(CONSTANTS_AT, ("constants",))]
    for c in range(NCH):
        for (name, *at), pos in STAGE1.items():
            step = (name, c, *at) if name == "amplify" else (name, *at, c)
            out.append((FIRST.get((name, *at), pos) if c == 0 else 8 * c + pos, step))
        for t in range(GT):
            out.append((8 * c + 2 * t, ("products", c, t)))
            out += [(8 * c + 2 * t + SHIFTED_AT + SHIFTED_STEP * half, ("shifted", 8 * c + 2 * t + half)) for half in range(2)]
    return [step for _, step in sorted(out, key=lambda o: o[0])] + [("router",)]


def first_mixture(pairs):
    out = []
    for p in pairs:
        if p == pairs[0]:
            if p == 0:
                out.append(("select", 0))
            out += [("hidden0", 4 * p), ("hidden0", 4 * p + 1)]
            if p == 0:
                out += [("select_scaled", 0), ("select", 1)]
        for k in range(2):
            n = 4 * p + 2 * k + 2
            if n < 4 * (pairs[-1] + 1):
                out += [("hidden0", n), ("hidden0", n + 1)]
            if (p, k) == (1, 0):
                out.append(("select_scaled", 1))
            out.append(("down0", p, k))
    return out


NORM_AT = {
    "center": (0, 0),
    "root": (1, 0.25),
    "spread": (3, 0.3),
    "parts": (4, 0.3),
}
GATE_AT = {
    "logits": (0, 0.8),
    "gate": (1, 0.65),
    "turn": (5, 0.65),
}


def norm(i, g, late=True):
    at = NORM_AT
    out = [(at["root"][0], ("root", i, g))]
    for k in range(GCH):
        for name in ("center", "spread", "parts")[:3 if late else 2]:
            out.append((at[name][0] + k * at[name][1], (name, i, GCH * g + k)))
    return out


def gate_steps(g):
    at = GATE_AT
    return ([(at["logits"][0], ("logits", g))] + [(at["gate"][0] + k * at["gate"][1], ("gate", g, k)) for k in range(GATE_PIECES)]
            + [(at["turn"][0] + k * at["turn"][1], ("turn", g, k)) for k in range(3)])


def stages(g):
    return {"norm2": norm(2, g, late=False), "norm3": norm(3, g), "conv": [(k, ("conv", 4 * g + k)) for k in range(4)],
            "norm4": norm(4, g), "gate": gate_steps(g)}


def second_mixture(p):
    units = []
    for u in range(UNITS):
        e, kk = u // HID, u % HID
        unit = [("hidden", p, e, kk, 0), ("hidden", p, e, kk, 1)]
        if kk == HID - 1:
            unit.append(("gates", p, e))
        if u > 0:
            unit.append(("down", p, (u - 1) // HID, (u - 1) % HID))
        elif p > 0:
            unit.append(("down", p - 1, EXP - 1, HID - 1))
        units.append(unit)
    return units


GROUP0 = {
    "norm2": (-38, 1.5),
    "norm3": (-31, 1),
    "conv": (-24, 0.75),
    "norm4": (-18, 1),
    "gate": (-8, 0.75),
}
GROUP1 = {
    "norm2": (-25, 2),
    "norm3": (-17, 2),
    "conv": (-6, 1),
    "norm4": (2, 1),
    "gate": (9, 1),
}
MIXTURE0_AT, MIXTURE0_APART = -46, 1.5


def plan():
    steps = []
    for g, table in enumerate((GROUP0, GROUP1)):
        for name, todo in stages(g).items():
            first, scale = table[name]
            steps += [(first + scale * at, [step]) for at, step in todo]
    steps += [(MIXTURE0_AT + MIXTURE0_APART * k, [step]) for k, step in enumerate(first_mixture([2, 3]))]
    units = [unit for p in range(PAIRS) for unit in second_mixture(p)] + [[("down", PAIRS - 1, EXP - 1, HID - 1)]]
    steps += [(k, unit) for k, unit in enumerate(units)]
    out = first_stages() + first_mixture([0, 1])
    for _, step in sorted(steps, key=lambda o: o[0]):
        out += step
    return out


def build(nc, x, early_in, mix0_in, late_in, out):
    at_e, n_e = places(EARLY)
    at_m, n_m = places(MIX0)
    at_l, n_l = places(LATE)
    PLAN = plan()
    ctx = ExitStack()
    with ctx:
        def sb(name, shape, dt=F32):
            return ctx.enter_context(nc.sbuf_tensor(name, shape, dt))

        def sem(name):
            return ctx.enter_context(nc.semaphore(name))

        early = sb("early", [128, n_e])
        mix0 = sb("mix0", [128, n_m])
        late = sb("late", [128, n_l])

        def E(name, rows=128):
            return early[0:rows, at_e[name][0]:at_e[name][1]]

        def M(name, rows=128):
            return mix0[0:rows, at_m[name][0]:at_m[name][1]]

        def L(name, rows=128):
            return late[0:rows, at_l[name][0]:at_l[name][1]]

        w11_hl = sb("w11_hl", [128, 2, 128], F32R)
        perm_r = sb("perm_r", [128, GT, 128], F32R)
        l1sum_r = sb("l1sum_r", [128, 2], F32R)
        w1m_hl = sb("w1m_hl", [128, EXP, 2, F0], F32R)
        conv_hl = sb("conv_hl", [128, TAPS, 2, CH], F32R)
        wg_hl = sb("wg_hl", [128, 2, EXP], F32R)
        spread_r = sb("spread_r", [48, EXP, 128], F32R)
        w1_h = sb("w1_h", [128, EXP * F1], F32R)
        w1_l = sb("w1_l", [128, EXP * F1], F32R)

        X = sb("X", [128, COLS])
        D = sb("D", [128, COLS])
        Q = sb("Q", [128, COLS])
        N = sb("N", [128, COLS])
        XS = sb("XS", [128, 2, COLS], F32R)
        dev = sb("dev", [128, NT * 2])
        rdev = sb("rdev", [128, NT * 2])
        vary = sb("vary", [128, GN])
        work = sb("work", [128, GN])
        eps = sb("eps", [128, 2])
        bnw = sb("bnw", [128, 8])
        amp = sb("amp", [128, 2, COLS])
        amp_s = sb("amp_s", [128, 2, COLS], F32R)
        rl1 = sb("rl1", [128, NT * 2])
        rl1sq = sb("rl1sq", [128, NT * 2])
        h1 = sb("h1", [128, 4, PIX])
        gram = h1[:, :, 0:BANK]
        yraw = sb("yraw", [128, COLS])
        w1sel = amp_s[:, :, :].rearrange("p a n -> p (a n)")[:, 0:BATCH * 4 * F0].rearrange(
            "p (b k q f) -> p b k q f", b=BATCH, k=2, q=2)
        h0 = amp[:, 0, :].rearrange("p (s n) -> p s n", s=4)
        gB = amp[:, 0, 0:2 * PIX].rearrange("p (s n) -> p s n", s=2)
        tmp = amp[:, 0, 2 * PIX:3 * PIX]
        clow = amp[:, 1, :]
        imsum = sb("imsum", [128, PAIRS])
        msum = sb("msum", [128, BATCH])
        r8 = sb("r8", [8, 16, 8])
        pick = sb("pick", [8, 2, 8])
        pickv = sb("pickv", [8, 4])
        pickd = sb("pickd", [8, 2, BATCH, 2])
        pickb = sb("pickb", [128, 2 * BATCH * 2])
        picki = sb("picki", [1, BATCH * 2], I32)
        wdT = sb("wdT", [8, 8])
        b2sel = sb("b2sel", [128, PAIRS])
        w2sel = sb("w2sel", [128, BATCH, 2, CH])
        w2b1sel = sb("w2b1sel", [128, 4 * PAIRS, CH + 1])
        img = sb("img", [128, BATCH, PADN], F32R)
        lg, key, gcmp, gw, pick1 = (yraw[:, q * GN * EXP:(q + 1) * GN * EXP].rearrange("p (n e) -> p n e", e=EXP)
                                    for q in range(5))
        gmx = sb("gmx", [128, 3, GN])
        gT = amp_s[0:48, 0, :]

        PS = ctx.enter_context(nc.psum_tensor("PS", [128, 8, 512], F32))

        def pair(k, n=BANK, lo=0, hi=128):
            return PS[lo:hi, 2 * k:2 * k + 2, 0:n]

        def psum(bank):
            return PS[:, bank, 0:BANK]

        def cols(t, c):
            return t[:, chunk(c)]

        def icols(t, p, lo=0, hi=128):
            return t[lo:hi, p * PIX:(p + 1) * PIX].rearrange("p (j n) -> p j n", j=2)

        def two(t):
            return t.rearrange("p (j n) -> p j n", j=2)

        x_in = [sem(f"x_in{i}") for i in range(PAIRS)]
        early_ld, mix0_ld, late_ld = sem("early_ld"), sem("mix0_ld"), sem("late_ld")
        prep_r = sem("prep_r")
        prep_w11 = sem("prep_w11")
        bn_a, bn_b = sem("bn_a"), sem("bn_b")
        fold = sem("fold")
        epsset = sem("epsset")
        root = sem("root")
        LN = [{k: sem(f"ln{i}_{k}") for k in
               ("centered", "squared", "copied", "summed", "rooted", "inverted", "spread", "normed", "high", "low")}
              for i in range(5)]
        amp_mm, amp_done = sem("amp_mm"), sem("amp_done")
        amp_hi, amp_lo = sem("amp_hi"), sem("amp_lo")
        l1_mm, l1_max, l1_inv, l1_sq, l1_bc = sem("l1_mm"), sem("l1_max"), sem("l1_inv"), sem("l1_sq"), sem("l1_bc")
        shift_mm, gram_done, y_mm, y_copied = sem("shift_mm"), sem("gram_done"), sem("y_mm"), sem("y_copied")
        y_scaled, y_act, fc_mm, x1_done = sem("y_scaled"), sem("y_act"), sem("fc_mm"), sem("x1_done")
        m0_hi, m0_lo = sem("m0_hi"), sem("m0_lo")
        rt, rt_pe, rt_act = sem("rt"), sem("rt_pe"), sem("rt_act")
        msum0, im_sum = sem("msum0"), sem("im_sum")
        sel_w1, sel_w1p, sel_w2, sel_b1 = sem("sel_w1"), sem("sel_w1p"), sem("sel_w2"), sem("sel_b1")
        sel_w2p, sel_b1p = sem("sel_w2p"), sem("sel_b1p")
        f0_mm, f0_act, f0_out, f0_res = sem("f0_mm"), sem("f0_act"), sem("f0_out"), sem("f0_res")
        xbeta, x2_done = sem("xbeta"), sem("x2_done")
        img0 = sem("img0")
        conv_w = sem("conv_w")
        conv_mm, conv_low, conv_a, x3_done = sem("conv_mm"), sem("conv_low"), sem("conv_a"), sem("x3_done")
        wg_s, w1_hs, w1_ls, spread_s = sem("wg_s"), sem("w1_hs"), sem("w1_ls"), sem("spread_s")
        lg_mm, gt, gt_act = sem("lg_mm"), sem("gt"), sem("gt_act")
        gT0, gT_mm, gT_hi, gT_lo = sem("gT0"), sem("gT_mm"), sem("gT_hi"), sem("gT_lo")
        f1_mm, f1_act = sem("f1_mm"), sem("f1_act")
        f1_out, o_mul, o_add = sem("f1_out"), sem("o_mul"), sem("o_add")
        stored = sem("stored")

        def ring_pair(n):
            return n % 2 if n < RING2 else (0, 1, 3)[(n - RING2) % 3]

        def hidden0_pair(n):
            return n % 2 if n < 8 else (1, 3)[n % 2]

        block = ctx.enter_context(nc.Block())

        @block.sync
        def _(sp):
            xv = x.rearrange("(h p) c y z -> p h c (y z)", h=2)
            ov = out.rearrange("(h p) c y z -> h c p (y z)", h=2)
            sp.dma_start(early[:, 0:at_e["w11"][0]], early_in[:, 0:at_e["w11"][0]]).then_inc(early_ld, 16)
            for p in range(PAIRS):
                for half in range(2):
                    sp.dma_start(X[64 * half:64 * half + 64, p * PIX:(p + 1) * PIX], xv[p, half]).then_inc(x_in[p], 16)
            sp.dma_start(early[:, at_e["w11"][0]:], early_in[:, at_e["w11"][0]:]).then_inc(early_ld, 16)
            sp.dma_start(mix0[:, :], mix0_in).then_inc(mix0_ld, 16)
            sp.dma_start(late[:, :], late_in).then_inc(late_ld, 16)
            for p in range(PAIRS):
                sp.wait_ge(o_add, EXP * (p + 1))
                for half in range(2):
                    sp.dma_start(ov[half][:, p], X[64 * half:64 * half + 64, p * PIX:(p + 1) * PIX]).then_inc(stored, 16)
            sp.wait_ge(stored, 16 * 2 * PAIRS)

        @block.tensor
        def _(pe):
            def center(i, c):
                if i == 0:
                    pe.wait_ge(early_ld, 16)
                    for p in range(images_for(c)):
                        pe.wait_ge(x_in[p], 32)
                    if c >= 3:
                        pe.wait_ge(LN[0]["normed"], (1, 4, 5)[c - 3])
                elif i == 1:
                    pe.wait_ge(x1_done, c + 1)
                    if c == 0:
                        pe.wait_ge(LN[0]["normed"], 2)
                    elif c == NCH - 1:
                        pe.wait_ge(LN[0]["normed"], NCH)
                    else:
                        pe.wait_ge(LN[1]["normed"], c)
                else:
                    g, k = c // GCH, c % GCH
                    if i == 2:
                        pe.wait_ge(f0_res, images_for(c))
                        pe.wait_ge(f0_act, (4 * PAIRS // GROUPS) * (g + 1))
                    if i == 3:
                        pe.wait_ge(x2_done, c + 1)
                    if i == 4:
                        pe.wait_ge(x3_done, images_for(c))
                        if g == 1:
                            pe.wait_ge(conv_a, 4 * GROUPS)
                    if k < 2 and i > 2:
                        pe.wait_ge(LN[i - 1]["normed"], GCH * g + k + 2)
                    if k == 2:
                        pe.wait_ge(LN[i]["squared"], c - 1)
                        pe.wait_ge(LN[i]["copied"], c - 1)
                pe.matmul(psum(ln_bank(i, c)), E("center"), X[:, chunk(c)], start=True, stop=True).then_inc(LN[i]["centered"], 1)

            def square_sums(bank, ts):
                for t in ts:
                    mm = pe.matmul(PS[:, bank, BANK + 2 * t:BANK + 2 * t + 2], Q[:, t * TILE:(t + 1) * TILE],
                                   E("blockmean"), start=True, stop=True)
                return mm

            def sums(i, c):
                pe.wait_ge(LN[i]["squared"], c + 1)
                pe.wait_ge(LN[i]["copied"], c + 1)
                square_sums(ln_bank(i, c), tiles(c)).then_inc(LN[i]["summed"], 1)

            def root_(i, g):
                c = GCH * g + 1
                pe.wait_ge(LN[i]["squared"], c + 2)
                pe.wait_ge(LN[i]["copied"], c + 1)
                square_sums(ln_bank(i, c), range(GTILES * g, GTILES * (g + 1))).then_inc(LN[i]["summed"], 1)

            def spread(i, c):
                if i < 2:
                    pe.wait_ge(LN[i]["inverted"], c + 1)
                else:
                    pe.wait_ge(LN[i]["inverted"], c // GCH + 1)
                    if c % GCH == 0:
                        pe.wait_ge(LN[i]["copied"], c + GCH)
                    if c % GCH == GCH - 1:
                        pe.wait_ge(LN[i]["normed"], c - 1)
                for k, t in enumerate(tiles(c)):
                    for half in range(2):
                        n = 2 * t + half
                        mm = pe.matmul(PS[64 * half:64 * half + 64, ln_bank(i, c), k * TILE:(k + 1) * TILE],
                                       rdev[:, n:n + 1].to_broadcast([128, CH]), E("ident"), start=True, stop=True,
                                       skip_group_check=True)
                mm.then_inc(LN[i]["spread"], 1)

            def amplify(c, half):
                n = 2 * c + half
                pe.wait_ge(prep_w11, 2)
                pe.wait_ge(LN[0]["high"], c + 1)
                pe.wait_ge(LN[0]["low"], c + 1)
                if n > 0:
                    pe.wait_ge(amp_done, n)
                    pe.wait_ge(amp_hi, n)
                if half == 0 and c > 0:
                    pe.wait_ge(l1_max, c)
                for part in range(2):
                    mm = pe.matmul(psum(2), w11_hl[:, part, :], XS[:, half, chunk(c)], start=part == 0, stop=part == 1)
                mm.then_inc(amp_mm, 1)

            def l1(c):
                pe.wait_ge(prep_r, 2)
                pe.wait_ge(amp_lo, 2 * c + 2)
                pe.wait_ge(amp_done, 2 * c + 2)
                pe.wait_ge(amp_hi, 2 * c + 2)
                for t in tiles(c):
                    for half in range(2):
                        mm = pe.matmul(PS[:, 2, BANK + 4 * (t - CT * c) + 2 * half:BANK + 4 * (t - CT * c) + 2 * half + 2],
                                       amp_s[:, half, t * TILE:(t + 1) * TILE], l1sum_r[:, :], start=True, stop=True)
                mm.then_inc(l1_mm, 1)

            def shifted(n):
                c, t, half = n // 8, n // 2 % 4, n % 2
                pe.wait_ge(prep_r, 2)
                pe.wait_ge(amp_lo, 2 * c + half + 1)
                pe.wait_ge(amp_hi, 2 * c + half + 1)
                if n >= 3:
                    pe.wait_ge(gram_done, n - 2)
                pe.matmul(psum(SHIFT_BANK[n % 3]), perm_r[:, t, :], amp_s[:, half, chunk(c)], start=True, stop=True).then_inc(shift_mm, 1)

            def products(c, t):
                pe.wait_ge(gram_done, 8 * c + 2 * t + 2)
                if t == 0 and c > 0:
                    pe.wait_ge(y_copied, c)
                w = E("w12").rearrange("p (t o) -> p t o", t=GT)[:, t]
                for half in range(2):
                    mm = pe.matmul(PS[64 * half:64 * half + 64, 4, 0:BANK], w, gram[:, 2 * (t % 2) + half, :],
                                   start=t == 0, stop=t == GT - 1, skip_group_check=True)
                mm.then_inc(y_mm, 1)

            def spread_l1(c):
                pe.wait_ge(l1_sq, c + 1)
                if c == 0:
                    pe.wait_ge(LN[0]["normed"], 3)
                else:
                    pe.wait_ge(x1_done, c)
                for k, t in enumerate(tiles(c)):
                    for half in range(2):
                        n = 2 * t + half
                        mm = pe.matmul(PS[64 * half:64 * half + 64, 5, k * TILE:(k + 1) * TILE],
                                       rl1sq[:, n:n + 1].to_broadcast([128, CH]), E("ident"), start=True, stop=True,
                                       skip_group_check=True)
                mm.then_inc(l1_bc, 1)

            def fc(c):
                pe.wait_ge(y_act, c + 1)
                pe.matmul(psum(5), E("wfcx"), N[:, chunk(c)], start=True, stop=False)
                pe.matmul(psum(5), E("wfcy"), yraw[:, chunk(c)], start=False, stop=True).then_inc(fc_mm, 1)

            def router():
                pe.wait_ge(mix0_ld, 16)
                pe.wait_ge(rt, RT_SUM)
                pe.matmul(PS[0:8, 4, 0:8], msum[:, :], M("wr"), start=True, stop=True).then_inc(rt_pe, 1)
                pe.wait_ge(rt, RT_SOFT1)
                pe.matmul(PS[0:8, 4, 8:16], M("ones8", 8)[:, 0:8], r8[:, 4, :], start=True, stop=True).then_inc(rt_pe, 1)
                pe.wait_ge(rt, RT_PICKED)
                pe.matmul(PS[:, 4, 16:48], M("ones8", 8), pickd[:, :, :, :].rearrange("p a b c -> p (a b c)"),
                          start=True, stop=True).then_inc(rt_pe, 1)
                pe.matmul(PS[0:8, 5, 0:8], r8[:, 14, :], M("eye8", 8), start=True, stop=True).then_inc(rt_pe, 1)
                pe.wait_ge(rt, RT_WDT)
                for half in range(2):
                    mm = pe.matmul(PS[64 * half:64 * half + 64, 5, 16:16 + PAIRS], M("b2", 8), wdT[:, PAIRS * half:PAIRS * half + PAIRS],
                                   start=True, stop=True, skip_group_check=True)
                mm.then_inc(rt_pe, 1)

            def hidden0(n):
                p, k, half = n // 4, n // 2 % 2, n % 2
                b = PAIRS * half + p
                pe.wait_ge((sel_w1, sel_w1p)[half], 2 * p + k + 1)
                pe.wait_ge(LN[1]["low"], 2 * chunks_for(p))
                pe.wait_ge(LN[1]["high"], chunks_for(p))
                if n == 8:
                    pe.wait_ge(f0_act, 8)
                elif n >= 2 and n != 9:
                    pe.wait_ge(f0_act, n - 1)
                for j in range(2):
                    a = p * PIX + j * HALFPIX
                    for part in range(2):
                        mm = pe.matmul(PS[:, 2 * hidden0_pair(n) + j, 0:HALFPIX], w1sel[:, b, k, part, :], XS[:, half, a:a + HALFPIX],
                                       start=part == 0, stop=part == 1)
                mm.then_inc(f0_mm, 1)

            def down0(p, k):
                pe.wait_ge(f0_act, 4 * p + 2 * k + 2)
                pe.wait_ge((sel_w2, sel_w2p)[p // 2], 2 * (2 * (p % 2) + 1) + k + 1)
                if k == 0:
                    if p == 0:
                        pe.wait_ge(rt, RT_B2)
                    else:
                        pe.wait_ge(f0_res, p)
                for j in range(2):
                    for half in range(2):
                        mm = pe.matmul(PS[64 * half:64 * half + 64, 4 + j, 0:HALFPIX], w2sel[:, PAIRS * half + p, k, :],
                                       h0[:, 2 * k + half, j * HALFPIX:(j + 1) * HALFPIX], start=k == 0, stop=k == 1,
                                       skip_group_check=True)
                mm.then_inc(f0_out, 1)

            def conv(n):
                p, half = n // 2, n % 2
                k = CONV_PAIR[n]
                pe.wait_ge(conv_w, 2)
                pe.wait_ge(LN[3]["high"], chunks_for(p))
                pe.wait_ge(LN[3]["low"], chunks_for(p))
                if n == 0:
                    pe.wait_ge(f0_act, 4 * PAIRS)
                elif n == 1:
                    pe.wait_ge(f0_res, PAIRS)
                elif n < 4:
                    pe.wait_ge(conv_a, n - 1)
                elif n == 4:
                    pe.wait_ge(LN[3]["normed"], NCH)
                else:
                    pe.wait_ge(conv_a, n)
                iv = img[:, PAIRS * half + p, :].rearrange("p (y z) -> p y z", z=PADW)
                for j in range(2):
                    for tap in range(TAPS):
                        dy, dx = tap // 3, tap % 3
                        mm = pe.matmul(PS[:, 2 * k + j, 0:HALFPIX], conv_hl[:, tap, :, :].rearrange("p a o -> p (a o)"),
                                       iv[:, j * ROWS + dy:j * ROWS + dy + ROWS, dx:dx + WD],
                                       start=tap == 0, stop=tap == TAPS - 1)
                mm.then_inc(conv_mm, 1)

            def logits(g):
                pe.wait_ge(wg_s, 2)
                pe.wait_ge(conv_a, 4 * (g + 1))
                pe.wait_ge(LN[4]["normed"], GCH * (g + 1))
                for t in range(GTILES * g, GTILES * (g + 1)):
                    if t % CT == 0:
                        pe.wait_ge(LN[4]["high"], t // CT + 1)
                        pe.wait_ge(LN[4]["low"], t // CT + 1)
                    for half in range(2):
                        n = 2 * (t - GTILES * g) + half
                        mm = pe.matmul(PS[:, LOGIT_BANK[g], 2 * EXP * n:2 * EXP * (n + 1)], XS[:, half, t * TILE:(t + 1) * TILE],
                                       wg_hl[:, :, :].rearrange("p a e -> p (a e)"), start=True, stop=True)
                mm.then_inc(lg_mm, 1)

            def turn(g, q):
                pe.wait_ge(gt, GT_ALL * (g + 1))
                if q == 2:
                    pe.wait_ge(gT_lo, 3 * g + 1)
                for k in range(3):
                    t = 3 * q + k
                    mm = pe.matmul(PS[0:16, TURN_BANK[g][q], k * TILE:(k + 1) * TILE],
                                   gw[:, 2 * t:2 * t + 2, :].rearrange("p a e -> p (a e)"), E("ident"), start=True, stop=True)
                mm.then_inc(gT_mm, 1)

            def slot_free(n):
                if n < 2:
                    pe.wait_ge(gt, GT_LOGITS)
                    pe.wait_ge(LN[4]["normed"], GCH)
                elif n == RING2 + 2:
                    pe.wait_ge(gT_lo, 6)
                elif n < RING2 + 2:
                    pe.wait_ge(f1_act, n - 1)
                else:
                    pe.wait_ge(f1_act, n - 2)

            def gates(p, e):
                n = UNITS_OF_RING * p + 5 * e + 4
                pe.wait_ge(spread_s, 1)
                pe.wait_ge(gT_lo, 3 if p < 2 else 6)
                pe.wait_ge(gT_hi, 3 if p < 2 else 6)
                slot_free(n)
                for j in range(2):
                    a = p * PIX + j * HALFPIX
                    mm = pe.matmul(PS[:, 2 * ring_pair(n) + j, 0:HALFPIX], spread_r[:, e, :], gT[:, a:a + HALFPIX],
                                   start=True, stop=True)
                mm.then_inc(f1_mm, 1)

            def hidden(p, e, kk, half):
                n = UNITS_OF_RING * p + 5 * e + 2 * kk + half
                pe.wait_ge(w1_hs, 1)
                pe.wait_ge(w1_ls, 1)
                pe.wait_ge(LN[4]["high"], chunks_for(p))
                pe.wait_ge(LN[4]["low"], chunks_for(p))
                slot_free(n)
                u = e * F1 + kk * 128
                for j in range(2):
                    a = p * PIX + j * HALFPIX
                    o = PS[:, 2 * ring_pair(n) + j, 0:HALFPIX]
                    pe.matmul(o, w1_h[:, u:u + 128], XS[:, half, a:a + HALFPIX], start=True, stop=False)
                    mm = pe.matmul(o, w1_l[:, u:u + 128], XS[:, half, a:a + HALFPIX], start=False, stop=True)
                mm.then_inc(f1_mm, 1)

            def down(p, e, kk):
                n = EXP * p + e
                pe.wait_ge(f1_act, UNITS_OF_RING * p + 5 * e + 2 * kk + 2)
                if kk == 0:
                    if n == 0:
                        pe.wait_ge(gT_lo, 3)
                    else:
                        pe.wait_ge(o_mul, n)
                u = (HID * e + kk) * CH
                for j in range(2):
                    for half in range(2):
                        mm = pe.matmul(PS[64 * half:64 * half + 64, 4 + j, 0:HALFPIX], L("w2")[:, u:u + CH],
                                       h1[:, 2 * kk + half, j * HALFPIX:(j + 1) * HALFPIX], start=kk == 0, stop=kk == HID - 1,
                                       skip_group_check=True)
                mm.then_inc(f1_out, 1)

            part = {"center": center, "sums": sums, "root": root_, "spread": spread, "amplify": amplify, "l1": l1,
                    "shifted": shifted,
                    "products": products, "spread_l1": spread_l1, "fc": fc, "router": router, "hidden0": hidden0,
                    "down0": down0, "conv": conv, "logits": logits, "turn": turn, "gates": gates, "hidden": hidden,
                    "down": down}
            for name, *at in PLAN:
                if name in part:
                    part[name](*at)

        @block.scalar
        def _(act):
            def constants():
                act.wait_ge(early_ld, 32)
                act.activation(perm_r[:, :, :].rearrange("p t m -> p (t m)"), E("perm"), ACT.Copy).then_inc(prep_r, 1)
                act.activation(l1sum_r[:, :], E("l1sum"), ACT.Copy).then_inc(prep_r, 1)
                act.wait_ge(epsset, 1)
                act.activation(bnw[:, 0:1], E("bn1")[:, 3:4], ACT.Sqrt, bias=eps[:, 1:2]).then_inc(bn_a, 1)
                act.activation(bnw[:, 4:5], E("bn2")[:, 3:4], ACT.Sqrt, bias=eps[:, 1:2]).then_inc(bn_a, 1)

            def center(i, c):
                act.wait_ge(LN[i]["centered"], c + 1)
                act.activation(cols(Q, c), psum(ln_bank(i, c)), ACT.Square).then_inc(LN[i]["squared"], 1)
                act.activation(cols(D, c), psum(ln_bank(i, c)), ACT.Copy).then_inc(LN[i]["copied"], 1)

            def sums(i, c):
                act.wait_ge(epsset, 1)
                act.wait_ge(LN[i]["summed"], c + 1)
                a, b = 2 * tiles(c)[0], 2 * tiles(c)[-1] + 2
                act.activation(dev[:, a:b], PS[:, ln_bank(i, c), BANK + a:BANK + b], ACT.Sqrt,
                               bias=eps[:, i:i + 1]).then_inc(LN[i]["rooted"], 1)

            def parts(i, c):
                act.wait_ge(LN[i]["normed"], c + 1)
                if i == 3:
                    act.wait_ge(img0, 1)
                    for p, y0, ny in pieces(c):
                        a = p * PIX + y0 * WD
                        for half in range(2):
                            q = slice(64 * half, 64 * half + 64)
                            iv = img[q, PAIRS * half + p, :].rearrange("p (y z) -> p y z", z=PADW)
                            last = act.activation(iv[:, 1 + y0:1 + y0 + ny, 1:1 + WD],
                                                  N[q, a:a + ny * WD].rearrange("p (y z) -> p y z", z=WD), ACT.Copy)
                else:
                    if i == 1:
                        act.wait_ge(amp_mm, 2 * c + 2)
                    if i == 4:
                        act.wait_ge(f0_mm, 4 * PAIRS)
                    for half in range(2):
                        q = slice(64 * half, 64 * half + 64)
                        last = act.activation(XS[q, half, chunk(c)], N[q, chunk(c)], ACT.Copy)
                last.then_inc(LN[i]["high"], 1)

            def amplify(c, half):
                n = 2 * c + half
                act.wait_ge(fold, 2)
                act.wait_ge(amp_mm, n + 1)
                act.activation(amp_s[:, half, chunk(c)], psum(2), ACT.Relu, bias=bnw[:, 3:4],
                               scale=bnw[:, 2:3]).then_inc(amp_hi, 1)
                act.activation(amp[:, half, chunk(c)], psum(2), ACT.Relu, bias=bnw[:, 3:4],
                               scale=bnw[:, 2:3]).then_inc(amp_done, 1)

            def products(c, t):
                if t == GT - 1:
                    act.wait_ge(y_mm, GT * (c + 1))
                    act.activation(cols(yraw, c), psum(4), ACT.Copy).then_inc(y_copied, 1)

            def fc(c):
                act.wait_ge(y_scaled, c + 1)
                act.activation(cols(yraw, c), cols(yraw, c), ACT.Relu, bias=bnw[:, 7:8], scale=bnw[:, 6:7]).then_inc(y_act, 1)

            def router():
                act.wait_ge(rt, RT_L1)
                act.activation(r8[:, 3, :], r8[:, 0, :], ACT.Exp, bias=r8[:, 1, 0:1], accum_out=r8[:, 2, 0:1]).then_inc(rt_act, 1)
                act.wait_ge(rt, RT_L2)
                act.activation(r8[:, 7, :], r8[:, 5, :], ACT.Exp, bias=r8[:, 6, 0:1], accum_out=r8[:, 2, 1:2]).then_inc(rt_act, 1)
                act.wait_ge(rt, RT_DIFF)
                act.activation(r8[:, 12, 1:2], r8[:, 12, 0:1], ACT.Exp).then_inc(rt_act, 1)

            def select(p):
                act.wait_ge(rt, RT_IDX)
                w2b1 = M("w2b1").rearrange("p (e n) -> p e n", e=EXP)
                for half in range(2):
                    b = PAIRS * half + p
                    for k in range(2):
                        n = 2 * (2 * p + half) + k
                        e = act.value_load(picki[0:1, 2 * b + k:2 * b + k + 1], min_val=0, max_val=EXP - 1)
                        act.activation(w2b1sel[:, n, :], w2b1[:, bass.ds(e, 1), :], ACT.Copy).then_inc(sel_b1, 1)

            def select_scaled(p):
                for half in range(2):
                    b = PAIRS * half + p
                    for k in range(2):
                        n = 2 * (2 * p + half) + k
                        act.wait_ge(sel_b1, n + 1)
                        wk = pickb[:, 16 + 2 * b + k:16 + 2 * b + k + 1]
                        act.activation(w2sel[:, b, k, :], w2b1sel[:, n, 0:CH], ACT.Copy, scale=wk).then_inc(sel_w2, 1)

            def hidden0(n):
                p, k, half = n // 4, n // 2 % 2, n % 2
                act.wait_ge(f0_mm, n + 1)
                act.wait_ge((sel_b1, sel_b1p)[p // 2], 2 * (2 * (p % 2) + half) + k + 1)
                if n >= 4:
                    act.wait_ge(f0_out, 2 * (p - 1) + k + 1)
                act.activation(two(h0[:, 2 * k + half, :]), pair(hidden0_pair(n), HALFPIX), ACT.Gelu,
                               bias=w2b1sel[:, 2 * (2 * p + half) + k, CH:CH + 1]).then_inc(f0_act, 1)

            def conv(n):
                p, half = n // 2, n % 2
                act.wait_ge(conv_mm, n + 1)
                act.wait_ge(x2_done, chunks_for(p))
                act.activation(icols(clow, p, 64 * half, 64 * half + 64),
                               pair(CONV_PAIR[n], HALFPIX, 64 - 64 * half, 128 - 64 * half), ACT.Copy,
                               scale=1.0 / TAPS).then_inc(conv_low, 1)

            def gate(g, k):
                if k == 0:
                    act.wait_ge(gt, GT_ALL * g + GT_EXP)
                    act.activation(gw[:, :, :], gcmp[:, :, :], ACT.Exp).then_inc(gt_act, 1)

            def gates(p, e):
                n = EXP * p + e
                act.wait_ge(f1_mm, 5 * n + 5)
                if n >= 2:
                    act.wait_ge(o_mul, n - 1)
                act.activation(two(gB[:, e % 2, :]), pair(ring_pair(5 * n + 4), HALFPIX), ACT.Copy).then_inc(f1_act, 1)

            def hidden(p, e, kk, half):
                n = EXP * p + e
                s = 5 * n + 2 * kk + half
                act.wait_ge(late_ld, 16)
                act.wait_ge(f1_mm, s + 1)
                if n:
                    act.wait_ge(f1_out, HID * (n - 1) + kk + 1)
                act.activation(two(h1[:, 2 * kk + half, 0:PIX]), pair(ring_pair(s), HALFPIX), ACT.Gelu,
                               bias=L("b1")[:, HID * e + kk:HID * e + kk + 1]).then_inc(f1_act, 1)

            part = {"constants": constants, "center": center, "sums": sums, "parts": parts, "amplify": amplify,
                    "products": products, "fc": fc, "router": router, "select": select, "select_scaled": select_scaled, "hidden0": hidden0, "conv": conv, "gate": gate,
                    "gates": gates, "hidden": hidden}
            for name, *at in PLAN:
                if name in part:
                    part[name](*at)

        @block.gpsimd
        def _(pool):
            pool.memset(img[:, :, :].bitcast(F32).rearrange("p b n -> p (b n)"), 0.0).then_inc(img0, 1)
            pool.memset(msum[:, :], 0.0).then_inc(msum0, 1)
            def split(high, low, src, high_done, low_done):
                pool.tensor_copy(high, src).then_inc(high_done, 1)
                pool.wait_ge(high_done, 1)
                pool.tensor_tensor(low, src, high.bitcast(F32), ALU.subtract).then_inc(low_done, 1)

            pool.wait_ge(mix0_ld, 16)
            split(w1m_hl[:, :, 0, :], w1m_hl[:, :, 1, :], M("w1").rearrange("p (e f) -> p e f", e=EXP), m0_hi, m0_lo)
            pool.wait_ge(late_ld, 16)
            split(conv_hl[:, :, 0, :], conv_hl[:, :, 1, :], L("conv").rearrange("p (t o) -> p t o", t=TAPS), conv_w, conv_w)
            split(wg_hl[:, 0, :], wg_hl[:, 1, :], L("wg"), wg_s, wg_s)
            split(w1_h[:, :], w1_l[:, :], L("w1"), w1_hs, w1_ls)
            pool.tensor_copy(spread_r[:, :, :].rearrange("p e m -> p (e m)"), L("spread", 48)).then_inc(spread_s, 1)
            pool.wait_ge(spread_s, 1)
            for c in range(NCH):
                pool.wait_ge(LN[1]["high"], c + 1)
                pool.wait_ge(LN[1]["normed"], c + 1)
                for half in range(2):
                    q = slice(64 * half, 64 * half + 64)
                    o = slice(64 - 64 * half, 128 - 64 * half)
                    pool.tensor_tensor(XS[o, half, chunk(c)], N[q, chunk(c)], XS[q, half, chunk(c)].bitcast(F32),
                                       ALU.subtract).then_inc(LN[1]["low"], 1)
                    pool.wait_ge(LN[1]["low"], 2 * c + half + 1)
            pool.wait_ge(x1_done, NCH)
            pool.wait_ge(gram_done, 8 * NCH)
            pool.tensor_scalar(clow[:, :], X[:, :], M("beta"), None, ALU.add).then_inc(xbeta, 1)
            pool.wait_ge(m0_lo, 1)
            pool.wait_ge(rt, RT_IDX)
            for p in range(PAIRS):
                b = PAIRS + p
                for k in range(2):
                    e = pool.value_load(picki[0:1, 2 * b + k:2 * b + k + 1], min_val=0, max_val=EXP - 1)
                    pool.tensor_copy(w1sel[:, b, k, :, :], w1m_hl[:, bass.ds(e, 1), :, :].bitcast(F32)).then_inc(sel_w1p, 1)
            w2b1 = M("w2b1").rearrange("p (e n) -> p e n", e=EXP)
            for p in range(PAIRS // 2, PAIRS):
                for half in range(2):
                    b = PAIRS * half + p
                    for k in range(2):
                        n = 2 * (2 * (p - PAIRS // 2) + half) + k
                        e = pool.value_load(picki[0:1, 2 * b + k:2 * b + k + 1], min_val=0, max_val=EXP - 1)
                        pool.tensor_copy(w2b1sel[:, 2 * PAIRS + n, :], w2b1[:, bass.ds(e, 1), :]).then_inc(sel_b1p, 1)
                        pool.wait_ge(sel_b1p, n + 1)
                        wk = pickb[:, 16 + 2 * b + k:16 + 2 * b + k + 1]
                        pool.tensor_scalar(w2sel[:, b, k, :], w2b1sel[:, 2 * PAIRS + n, 0:CH], wk, None, ALU.mult).then_inc(sel_w2p, 1)
            pool.wait_ge(f0_mm, 4 * PAIRS)
            pool.memset(gT[0:32, :].bitcast(F32), 0.0).then_inc(gT0, 1)

        @block.vector
        def _(ve):
            ve.memset(eps[:, 0:1], 1e-6)
            ve.memset(eps[:, 1:2], 1e-5).then_inc(epsset, 1)
            step = {}

            def then(ins, s=rt):
                ins.then_inc(s, 1)
                step[s.name] = step.get(s.name, 0) + 1
                ve.wait_ge(s, step[s.name])

            def constants():
                ve.wait_ge(early_ld, 32)
                ve.tensor_copy(w11_hl[:, 0, :], E("w11")).then_inc(prep_w11, 1)
                ve.wait_ge(prep_w11, 1)
                ve.tensor_tensor(w11_hl[:, 1, :], E("w11"), w11_hl[:, 0, :].bitcast(F32), ALU.subtract).then_inc(prep_w11, 1)
                ve.wait_ge(bn_a, 2)
                for k, name in enumerate(("bn1", "bn2")):
                    g, b, m = (E(name)[:, q:q + 1] for q in range(3))
                    o = 4 * k
                    ve.reciprocal(bnw[:, o + 1:o + 2], bnw[:, o:o + 1]).then_inc(bn_b, 1)
                    ve.wait_ge(bn_b, 3 * k + 1)
                    ve.tensor_tensor(bnw[:, o + 2:o + 3], bnw[:, o + 1:o + 2], g, ALU.mult).then_inc(bn_b, 1)
                    ve.wait_ge(bn_b, 3 * k + 2)
                    ve.tensor_tensor(bnw[:, o + 1:o + 2], bnw[:, o + 2:o + 3], m, ALU.mult).then_inc(bn_b, 1)
                    ve.wait_ge(bn_b, 3 * k + 3)
                    ve.tensor_tensor(bnw[:, o + 3:o + 4], b, bnw[:, o + 1:o + 2], ALU.subtract).then_inc(fold, 1)

            def sums(i, c):
                ve.wait_ge(LN[i]["rooted"], c + 1)
                a, b = 2 * tiles(c)[0], 2 * tiles(c)[-1] + 2
                ve.reciprocal(rdev[:, a:b], dev[:, a:b]).then_inc(LN[i]["inverted"], 1)

            def root_(i, g):
                c = GCH * g + 1
                r = slice(GN * g, GN * (g + 1))
                ve.wait_ge(LN[i]["summed"], g + 1)
                src = PS[:, ln_bank(i, c), BANK + GN * g:BANK + GN * (g + 1)]
                then(ve.tensor_scalar(vary[:, :], src, 1e-6 if i == 3 else 1e-5, None, ALU.add), root)
                y = rdev[:, r]
                then(ve.tensor_scalar(y.bitcast(I32), vary[:, :].bitcast(I32), -0.5, float(0x5F3759DF), ALU.mult, ALU.add), root)
                for k in range(3):
                    then(ve.tensor_tensor(work[:, :], y, y, ALU.mult), root)
                    then(ve.scalar_tensor_tensor(out=work[:, :], in0=work[:, :], scalar=-0.5, in1=vary[:, :],
                                                 op0=ALU.mult, op1=ALU.mult), root)
                    last = ve.scalar_tensor_tensor(out=y, in0=work[:, :], scalar=1.5, in1=y, op0=ALU.add, op1=ALU.mult)
                    if k < 2:
                        then(last, root)
                last.then_inc(LN[i]["inverted"], 1)

            def spread(i, c):
                ve.wait_ge(LN[i]["spread"], c + 1)
                ve.wait_ge(LN[i]["copied"], c + 1)
                if i == 2:
                    ve.scalar_tensor_tensor(out=cols(N, c), in0=psum(ln_bank(i, c)), scalar=M("gamma"), in1=cols(D, c),
                                            op0=ALU.mult, op1=ALU.mult).then_inc(LN[2]["normed"], 1)
                    ve.wait_ge(xbeta, 1)
                    ve.wait_ge(LN[2]["normed"], c + 1)
                    ve.tensor_tensor(cols(X, c), cols(N, c), cols(clow, c), ALU.add).then_inc(x2_done, 1)
                else:
                    ve.tensor_tensor(cols(N, c), psum(ln_bank(i, c)), cols(D, c), ALU.mult).then_inc(LN[i]["normed"], 1)

            def image_sums(c):
                ve.wait_ge(LN[1]["normed"], c + 1)
                for p in range(images_in(c), images_in(c + 1)):
                    ve.tensor_reduce(imsum[:, p:p + 1], N[:, p * PIX:(p + 1) * PIX], AX, ALU.add).then_inc(im_sum, 1)

            def parts(i, c):
                if i == 1:
                    image_sums(c)
                    return
                ve.wait_ge(LN[i]["high"], c + 1)
                ve.wait_ge(LN[i]["normed"], c + 1)
                for half in range(2):
                    q = slice(64 * half, 64 * half + 64)
                    o = slice(64 - 64 * half, 128 - 64 * half)
                    if i == 3:
                        for p, y0, ny in pieces(c):
                            a = p * PIX + y0 * WD
                            hv = img[q, PAIRS * half + p, :].rearrange("p (y z) -> p y z", z=PADW)
                            lv = img[o, PAIRS * half + p, :].rearrange("p (y z) -> p y z", z=PADW)
                            last = ve.tensor_tensor(lv[:, 1 + y0:1 + y0 + ny, 1:1 + WD],
                                                    N[q, a:a + ny * WD].rearrange("p (y z) -> p y z", z=WD),
                                                    hv[:, 1 + y0:1 + y0 + ny, 1:1 + WD].bitcast(F32), ALU.subtract)
                    else:
                        r = chunk(c)
                        last = ve.tensor_tensor(XS[o, half, r], N[q, r], XS[q, half, r].bitcast(F32), ALU.subtract)
                last.then_inc(LN[i]["low"], 1)

            def amplify(c, half):
                n = 2 * c + half
                ve.wait_ge(amp_hi, n + 1)
                ve.wait_ge(amp_done, n + 1)
                low = amp_s[64:128, half, chunk(c)]
                ve.tensor_tensor(low, amp[64:128, half, chunk(c)], low.bitcast(F32), ALU.subtract).then_inc(amp_lo, 1)

            def l1(c):
                a, b = 2 * tiles(c)[0], 2 * tiles(c)[-1] + 2
                ve.wait_ge(l1_mm, c + 1)
                src = PS[:, 2, BANK:BANK + 4 * CT].rearrange("p (n two) -> p n two", two=2)[:, :, 0]
                ve.tensor_scalar(rl1[:, a:b], src, 1e-12, None, ALU.max).then_inc(l1_max, 1)
                ve.wait_ge(l1_max, c + 1)
                ve.reciprocal(rl1sq[:, a:b], rl1[:, a:b]).then_inc(l1_inv, 1)
                ve.wait_ge(l1_inv, c + 1)
                ve.tensor_tensor(rl1sq[:, a:b], rl1sq[:, a:b], rl1sq[:, a:b], ALU.mult).then_inc(l1_sq, 1)

            def shifted(n):
                c, t, half = n // 8, n // 2 % 4, n % 2
                ve.wait_ge(shift_mm, n + 1)
                if n >= 4:
                    ve.wait_ge(y_mm, n // 2 - 1)
                ve.tensor_tensor(gram[:, 2 * (t % 2) + half, :], psum(SHIFT_BANK[n % 3]), amp[:, half, chunk(c)],
                                 ALU.mult).then_inc(gram_done, 1)

            def spread_l1(c):
                ve.wait_ge(y_copied, c + 1)
                ve.wait_ge(l1_bc, c + 1)
                ve.tensor_tensor(cols(yraw, c), psum(5), cols(yraw, c), ALU.mult).then_inc(y_scaled, 1)

            def fc(c):
                ve.wait_ge(fc_mm, c + 1)
                ve.scalar_tensor_tensor(out=cols(X, c), in0=psum(5), scalar=E("bfc"), in1=cols(X, c),
                                        op0=ALU.add, op1=ALU.add).then_inc(x1_done, 1)

            def router():
                ve.wait_ge(msum0, 1)
                ve.wait_ge(im_sum, PAIRS)
                ve.tensor_copy(msum[0:64, 0:PAIRS], imsum[0:64, :])
                then(ve.tensor_copy(msum[64:128, PAIRS:BATCH], imsum[64:128, :]))
                ve.wait_ge(rt_pe, 1)
                then(ve.scalar_tensor_tensor(out=r8[:, 0, :], in0=PS[0:8, 4, 0:8], scalar=1.0 / PIX, in1=M("br", 8),
                                             op0=ALU.mult, op1=ALU.add))
                then(ve.tensor_reduce(r8[:, 1, 0:1], r8[:, 0, :], AX, ALU.max, negate=True))
                assert step[rt.name] == RT_L1
                ve.wait_ge(rt_act, 1)
                then(ve.reciprocal(r8[:, 1, 1:2], r8[:, 2, 0:1]))
                then(ve.tensor_scalar(r8[:, 4, :], r8[:, 3, :], r8[:, 1, 1:2], None, ALU.mult))
                assert step[rt.name] == RT_SOFT1
                ve.wait_ge(rt_pe, 2)
                then(ve.reciprocal(r8[:, 10, :], PS[0:8, 4, 8:16]))
                then(ve.tensor_scalar(r8[:, 10, :], r8[:, 10, :], CAPACITY / PIX, 1.0, ALU.mult, ALU.min))
                then(ve.tensor_tensor(r8[:, 5, :], r8[:, 4, :], r8[:, 10, :], ALU.mult))
                then(ve.tensor_reduce(r8[:, 6, 0:1], r8[:, 5, :], AX, ALU.max, negate=True))
                assert step[rt.name] == RT_L2
                ve.wait_ge(rt_act, 2)
                then(ve.reciprocal(r8[:, 1, 2:3], r8[:, 2, 1:2]))
                then(ve.tensor_scalar(r8[:, 8, :], r8[:, 7, :], r8[:, 1, 2:3], None, ALU.mult))
                value, order = r8[:, 8, :], M("order", 8)
                best, first, index = r8[:, 13, 0:2], r8[:, 13, 2:4], pickv[:, 0:2]
                then(ve.tensor_reduce(best[:, 0:1], value, AX, ALU.max))
                then(ve.scalar_tensor_tensor(out=r8[:, 11, :], in0=value, scalar=best[:, 0:1], in1=order, op0=ALU.is_equal,
                                             op1=ALU.mult))
                then(ve.tensor_reduce(first[:, 0:1], r8[:, 11, :], AX, ALU.max))
                then(ve.tensor_scalar(pick[:, 0, :], r8[:, 11, :], first[:, 0:1], None, ALU.is_equal))
                then(ve.scalar_tensor_tensor(out=r8[:, 9, :], in0=pick[:, 0, :], scalar=-FAR, in1=value, op0=ALU.mult,
                                             op1=ALU.add))
                then(ve.tensor_reduce(best[:, 1:2], r8[:, 9, :], AX, ALU.max))
                then(ve.tensor_tensor(r8[:, 12, 0:1], best[:, 1:2], best[:, 0:1], ALU.subtract))
                assert step[rt.name] == RT_DIFF
                then(ve.scalar_tensor_tensor(out=r8[:, 11, :], in0=r8[:, 9, :], scalar=best[:, 1:2], in1=order,
                                             op0=ALU.is_equal, op1=ALU.mult))
                then(ve.tensor_reduce(first[:, 1:2], r8[:, 11, :], AX, ALU.max))
                then(ve.tensor_scalar(pick[:, 1, :], r8[:, 11, :], first[:, 1:2], None, ALU.is_equal))
                then(ve.tensor_scalar(index, first, -1.0, float(EXP), ALU.mult, ALU.add))
                ve.wait_ge(rt_act, 3)
                then(ve.tensor_scalar(r8[:, 12, 2:3], r8[:, 12, 1:2], 1.0, None, ALU.add))
                then(ve.reciprocal(pickv[:, 2:3], r8[:, 12, 2:3]))
                then(ve.tensor_tensor(pickv[:, 3:4], r8[:, 12, 1:2], pickv[:, 2:3], ALU.mult))
                then(ve.tensor_scalar(r8[:, 15, :], pick[:, 0, :], pickv[:, 2:3], None, ALU.mult))
                then(ve.scalar_tensor_tensor(out=r8[:, 14, :], in0=pick[:, 1, :], scalar=pickv[:, 3:4], in1=r8[:, 15, :],
                                             op0=ALU.mult, op1=ALU.add))
                diag = M("diag", 8).rearrange("p (b k) -> p b k", b=BATCH)
                for q in range(2):
                    val = pickv[:, 2 * q:2 * q + 2].unsqueeze(1).to_broadcast([8, BATCH, 2])
                    then(ve.tensor_tensor(pickd[:, q, :, :], diag, val, ALU.mult))
                assert step[rt.name] == RT_PICKED
                ve.wait_ge(rt_pe, 3)
                then(ve.tensor_copy(pickb[:, :], PS[:, 4, 16:48]))
                then(ve.tensor_copy(picki[:, :], PS[0:1, 4, 16:32]))
                assert step[rt.name] == RT_IDX
                ve.wait_ge(rt_pe, 4)
                then(ve.tensor_copy(wdT[:, :], PS[0:8, 5, 0:8]))
                assert step[rt.name] == RT_WDT
                ve.wait_ge(rt_pe, 5)
                then(ve.tensor_copy(b2sel[:, :], PS[:, 5, 16:16 + PAIRS]))
                assert step[rt.name] == RT_B2
                ve.wait_ge(m0_lo, 1)
                for b in range(PAIRS):
                    for k in range(2):
                        e = ve.value_load(picki[0:1, 2 * b + k:2 * b + k + 1], min_val=0, max_val=EXP - 1)
                        ve.tensor_copy(w1sel[:, b, k, :, :], w1m_hl[:, bass.ds(e, 1), :, :].bitcast(F32)).then_inc(sel_w1, 1)
            def down0(p, k):
                if k == 1:
                    ve.wait_ge(f0_out, 2 * p + 2)
                    ve.wait_ge(xbeta, 1)
                    ve.scalar_tensor_tensor(out=icols(X, p), in0=pair(2, HALFPIX), scalar=b2sel[:, p:p + 1],
                                            in1=icols(N, p), op0=ALU.add, op1=ALU.add).then_inc(f0_res, 1)

            def conv(n):
                p, half = n // 2, n % 2
                q = (64 * half, 64 * half + 64)
                ve.wait_ge(conv_low, n + 1)
                ve.scalar_tensor_tensor(out=icols(clow, p, *q), in0=pair(CONV_PAIR[n], HALFPIX, *q), scalar=1.0 / TAPS,
                                        in1=icols(clow, p, *q), op0=ALU.mult, op1=ALU.add).then_inc(conv_a, 1)
                if half == 1:
                    ve.wait_ge(conv_a, 2 * p + 2)
                    ve.tensor_tensor(icols(X, p), icols(X, p), icols(clow, p), ALU.add).then_inc(x3_done, 1)

            def gate(g, k):
                wide = [128, GN, EXP]
                order = L("order").unsqueeze(1).to_broadcast(wide)
                if k == 0:
                    ve.wait_ge(lg_mm, g + 1)
                    if g:
                        ve.wait_ge(gT_mm, 3)
                    both = PS[:, LOGIT_BANK[g], 0:2 * GN * EXP].rearrange("p (n a e) -> p n a e", a=2, e=EXP)
                    then(ve.tensor_tensor(lg[:, :, :], both[:, :, 1], L("bg").unsqueeze(1).to_broadcast(wide), ALU.add), gt)
                    then(ve.tensor_tensor(lg[:, :, :], both[:, :, 0], lg[:, :, :], ALU.add), gt)
                    then(ve.tensor_reduce(gmx[:, 0, :], lg[:, :, :], AX, ALU.max), gt)
                    then(ve.tensor_tensor(gcmp[:, :, :], lg[:, :, :], gmx[:, 0, :].unsqueeze(2).to_broadcast(wide),
                                          ALU.subtract), gt)
                elif k == 1:
                    then(ve.scalar_tensor_tensor(out=key[:, :, :], in0=gcmp[:, :, :], scalar=0.0, in1=order, op0=ALU.is_equal,
                                                 op1=ALU.mult), gt)
                    then(ve.tensor_reduce(gmx[:, 1, :], key[:, :, :], AX, ALU.max), gt)
                    then(ve.tensor_tensor(pick1[:, :, :], key[:, :, :], gmx[:, 1, :].unsqueeze(2).to_broadcast(wide),
                                          ALU.is_equal), gt)
                    then(ve.scalar_tensor_tensor(out=lg[:, :, :], in0=pick1[:, :, :], scalar=-FAR, in1=lg[:, :, :],
                                                 op0=ALU.mult, op1=ALU.add), gt)
                elif k == 2:
                    then(ve.tensor_reduce(gmx[:, 0, :], lg[:, :, :], AX, ALU.max), gt)
                    then(ve.tensor_tensor(key[:, :, :], lg[:, :, :], gmx[:, 0, :].unsqueeze(2).to_broadcast(wide),
                                          ALU.is_equal), gt)
                    then(ve.tensor_tensor(key[:, :, :], key[:, :, :], order, ALU.mult), gt)
                    then(ve.tensor_reduce(gmx[:, 1, :], key[:, :, :], AX, ALU.max), gt)
                    then(ve.tensor_tensor(key[:, :, :], key[:, :, :], gmx[:, 1, :].unsqueeze(2).to_broadcast(wide),
                                          ALU.is_equal), gt)
                    then(ve.tensor_tensor(pick1[:, :, :], pick1[:, :, :], key[:, :, :], ALU.add), gt)
                else:
                    ve.wait_ge(gt_act, g + 1)
                    then(ve.tensor_tensor(gw[:, :, :], gw[:, :, :], pick1[:, :, :], ALU.mult), gt)
                    then(ve.tensor_reduce(gmx[:, 1, :], gw[:, :, :], AX, ALU.add), gt)
                    then(ve.reciprocal(gmx[:, 2, :], gmx[:, 1, :]), gt)
                    then(ve.tensor_tensor(gw[:, :, :], gw[:, :, :], gmx[:, 2, :].unsqueeze(2).to_broadcast(wide), ALU.mult), gt)
                    assert step[gt.name] == GT_ALL * (g + 1)

            def turn(g, q):
                n = 3 * g + q
                r = slice(GCOLS * g + BANK * q, GCOLS * g + BANK * (q + 1))
                src = PS[0:16, TURN_BANK[g][q], 0:BANK]
                ve.wait_ge(gT0, 1)
                ve.wait_ge(gT_mm, n + 1)
                ve.tensor_copy(gT[0:16, r], src).then_inc(gT_hi, 1)
                ve.wait_ge(gT_hi, n + 1)
                ve.tensor_tensor(gT[32:48, r], src, gT[0:16, r].bitcast(F32), ALU.subtract).then_inc(gT_lo, 1)

            def down(p, e, kk):
                if kk == HID - 1:
                    n = EXP * p + e
                    ve.wait_ge(f1_out, HID * n + HID)
                    ve.wait_ge(f1_act, 5 * n + 5)
                    if n:
                        ve.wait_ge(o_add, n)
                    ve.scalar_tensor_tensor(out=two(tmp), in0=pair(2, HALFPIX), scalar=L("b2")[:, e:e + 1],
                                            in1=two(gB[:, e % 2, :]), op0=ALU.add, op1=ALU.mult).then_inc(o_mul, 1)
                    ve.wait_ge(o_mul, n + 1)
                    ve.tensor_tensor(icols(X, p), two(tmp), icols(X, p), ALU.add).then_inc(o_add, 1)

            part = {"constants": constants, "sums": sums, "root": root_, "spread": spread, "parts": parts,
                    "amplify": amplify, "l1": l1, "shifted": shifted, "spread_l1": spread_l1, "fc": fc,
                    "router": router, "down0": down0, "conv": conv, "gate": gate, "turn": turn, "down": down}
            for name, *at in PLAN:
                if name in part:
                    part[name](*at)


def halves(a):
    return np.concatenate([a, a], axis=0)


def column(v):
    return np.reshape(v, (-1, 1))


def blockdiag(a):
    out = np.zeros((128, 128), np.float32)
    out[0:64, 0:64] = a
    out[64:128, 64:128] = a
    return out


def pack(table, parts):
    at, n = places(table)
    out = np.zeros((128, n), np.float32)
    for name, (a, b) in at.items():
        part = np.asarray(parts[name])
        part = part.reshape(part.shape[0], -1)
        out[0:part.shape[0], a:b] = part
    return out


def shift_of(t, s):
    return GT * t + s + 1


def gram_weights(w12):
    first, second = np.triu_indices(MID, k=1)
    number = np.zeros((MID, MID), np.int64)
    number[first, second] = np.arange(len(first))
    out = np.zeros((128, GT, CH), np.float32)
    for t in range(GT):
        for s in range(4):
            d = shift_of(t, s)
            for i in range(MID if d < MID // 2 else MID // 2):
                j = (i + d) % MID
                out[MID * s + i, t] = w12[:, number[min(i, j), max(i, j)]]
    return out


def shift_matrices():
    out = np.zeros((128, GT, 128), np.float32)
    for t in range(GT):
        for s in range(4):
            for i in range(MID):
                j = (i + shift_of(t, s)) % MID
                out[j, t, MID * s + i] = 1
                out[64 + j, t, MID * s + i] = 1
    return out


def spread_matrices():
    out = np.zeros((48, EXP, 128), np.float32)
    for e in range(EXP):
        for half in range(2):
            for part in range(2):
                out[32 * part + EXP * half + e, e, 64 * half:64 * half + 64] = 1
    return out


def packed(v):
    blockmean = np.zeros((128, 2), np.float32)
    blockmean[0:64, 0] = 1 / CH
    blockmean[64:128, 1] = 1 / CH
    diag = np.zeros((8, BATCH, 2), np.float32)
    diag[np.arange(8), np.arange(8)] = 1
    early = pack(EARLY, {
        "center": blockdiag(np.eye(CH, dtype=np.float32) - np.float32(1 / CH)),
        "blockmean": blockmean,
        "ident": np.eye(128, dtype=np.float32),
        "w11": halves(np.concatenate([v["L0_conv_w11"].T] * 4, axis=1)),
        "bn1": np.concatenate([np.stack([v[f"L0_conv_{q}1"] for q in "gbmv"], axis=1)] * 4, axis=0),
        "bn2": halves(np.stack([v[f"L0_conv_{q}2"] for q in "gbmv"], axis=1)),
        "bfc": halves(column(v["L0_conv_bfc"])),
        "l1sum": np.full((128, 2), 0.5, np.float32),
        "perm": shift_matrices(),
        "w12": gram_weights(v["L0_conv_w12"]),
        "wfcy": blockdiag(v["L0_conv_wfc"][:, 0:CH].T),
        "wfcx": blockdiag(v["L0_conv_wfc"][:, CH:2 * CH].T),
    })
    mix0 = pack(MIX0, {
        "wr": halves(v["L0_ffn_Wr"]),
        "br": np.stack([v["L0_ffn_br"]] * 8),
        "order": np.stack([EXP - np.arange(EXP, dtype=np.float32)] * 8),
        "eye8": np.eye(8, dtype=np.float32),
        "diag": diag,
        "ones8": np.ones((8, 128), np.float32),
        "b2": v["L0_ffn_b2"],
        "gamma": halves(column(v["L0_ffn_gamma"])),
        "beta": halves(column(v["L0_ffn_beta"])),
        "w1": halves(v["L0_ffn_W1"].transpose(1, 0, 2)),
        "w2b1": np.concatenate([v["L0_ffn_W2"].transpose(1, 0, 2), v["L0_ffn_b1"].T[:, :, None]], axis=2),
    })
    late = pack(LATE, {
        "conv": halves(v["L1_conv_w"].reshape(CH, CH, TAPS).transpose(1, 2, 0)),
        "wg": halves(v["L1_ffn_Wg"]),
        "bg": np.stack([v["L1_ffn_bg"]] * 128),
        "order": np.stack([EXP - np.arange(EXP, dtype=np.float32)] * 128),
        "spread": spread_matrices(),
        "b1": v["L1_ffn_b1"].reshape(UNITS, 128).T,
        "b2": halves(v["L1_ffn_b2"].T),
        "w1": halves(v["L1_ffn_W1"].transpose(1, 0, 2)),
        "w2": v["L1_ffn_W2"].reshape(UNITS, 128, CH).transpose(1, 0, 2),
    })
    return early, mix0, late


def kernel(**inputs):
    import concourse.bacc as bacc
    from concourse.bass_utils import run_bass_kernel_spmd

    v = {name: np.asarray(a) for name, a in inputs.items()}
    early, mix0, late = packed(v)
    arrays = {"x_in": np.ascontiguousarray(v["x"]), "early_in": early, "mix0_in": mix0, "late_in": late}
    nc = bacc.Bacc("TRN2", target_bir_lowering=False, num_devices=1)
    aps = [nc.dram_tensor(name, a.shape, F32, kind="ExternalInput").ap() for name, a in arrays.items()]
    out = nc.dram_tensor("out", (BATCH, CH, HT, WD), F32, kind="ExternalOutput").ap()
    build(nc, *aps, out)
    return run_bass_kernel_spmd(nc, [arrays], core_ids=[0]).results[0]["out"]
```
